# Optimizing a Trainium2 kernel written in Bass

```python
import numpy as np
import jax
import jax.numpy as jnp

def _softmax(x, axis=-1):
    return jax.nn.softmax(x, axis=axis)

def _gelu(x):
    return jax.nn.gelu(x, approximate=True)

def _silu(x):
    return jax.nn.silu(x)

def _sigmoid(x):
    return jax.nn.sigmoid(x)

def _layernorm(x, axis=-1, eps=1e-05):
    m = jnp.mean(x, axis=axis, keepdims=True)
    v = jnp.var(x, axis=axis, keepdims=True)
    return (x - m) / jnp.sqrt(v + eps)

def _scatter_add(tgt, idx, src, axis=0):
    return tgt.at[idx].add(src)

def _segment_sum(src, seg, n):
    return jax.ops.segment_sum(src, seg, n)
kernel_name = 'mk_macaron_d1_jaxref_r4_947a31'

def setup_inputs(seed: int=0):
    np.random.seed(seed)
    _w = jnp.asarray

    def _L0_attn_setup():
        import jax, jax.numpy as jnp
        import numpy as np
        H = 32
        HKV = 8
        D = 1024
        HD = D // H
        S = 256
        MASK_OUT = 0.9
        MIN_REMAIN = 128
        THETA = 10000.0

        def rope_tables(seq_len, hd):
            inv_freq = 1.0 / THETA ** (jnp.arange(0, hd, 2, dtype=jnp.float32) / hd)
            t = jnp.arange(seq_len, dtype=jnp.float32)
            freqs = jnp.outer(t, inv_freq)
            emb = jnp.concatenate([freqs, freqs], axis=-1)
            return (jnp.cos(emb), jnp.sin(emb))

        def rotate_half(x):
            x1, x2 = jnp.split(x, 2, axis=-1)
            return jnp.concatenate([-x2, x1], axis=-1)

        def apply_rope(x, cos, sin):
            return x * cos + rotate_half(x) * sin
        key = jax.random.key(seed)
        k0, k1, k2, k3, k4 = jax.random.split(key, 5)
        hidden_states = jax.random.normal(k0, (1, S, D), jnp.float32)
        Wq = jax.random.normal(k1, (D, D), jnp.float32) * 0.02
        Wk = jax.random.normal(k2, (HKV * HD, D), jnp.float32) * 0.02
        Wv = jax.random.normal(k3, (HKV * HD, D), jnp.float32) * 0.02
        Wo = jax.random.normal(k4, (D, D), jnp.float32) * 0.02
        return {'hidden_states': hidden_states, 'Wq': Wq, 'Wk': Wk, 'Wv': Wv, 'Wo': Wo}
    _L0_attn_in = _L0_attn_setup()

    def _L0_ffn_setup():
        import jax, jax.numpy as jnp
        import numpy as np
        K_TOP = 8
        key = jax.random.key(seed)
        k1, k2, k3 = jax.random.split(key, 3)
        B, S, H, E = (4, 1024, 1024, 64)
        hidden_states = jax.random.normal(k1, (B, S, H), dtype=jnp.float32)
        router_weight = jax.random.normal(k2, (E, H), dtype=jnp.float32)
        router_bias = jnp.zeros((E,), dtype=jnp.float32)
        expert_bias = jax.random.normal(k3, (E, H), dtype=jnp.float32) * 0.1
        return {'hidden_states': hidden_states, 'router_weight': router_weight, 'router_bias': router_bias, 'expert_bias': expert_bias}
    _L0_ffn_in = _L0_ffn_setup()
    _d = {'L0_attn_hidden_states': _L0_attn_in['hidden_states'], 'L0_attn_Wq': _L0_attn_in['Wq'], 'L0_attn_Wk': _L0_attn_in['Wk'], 'L0_attn_Wv': _L0_attn_in['Wv'], 'L0_attn_Wo': _L0_attn_in['Wo'], 'L0_ffn_router_weight': _L0_ffn_in['router_weight'], 'L0_ffn_router_bias': _L0_ffn_in['router_bias'], 'L0_ffn_expert_bias': _L0_ffn_in['expert_bias']}
    _x0 = _d['L0_attn_hidden_states']
    _d['L0_attn_hidden_states'] = jax.random.normal(jax.random.fold_in(jax.random.key(seed), 1), (1, 2048, 1024), dtype=_x0.dtype)
    del _x0
    return _d

def reference(L0_attn_hidden_states, L0_attn_Wq, L0_attn_Wk, L0_attn_Wv, L0_attn_Wo, L0_ffn_router_weight, L0_ffn_router_bias, L0_ffn_expert_bias):

    def _L0_attn_ref(hidden_states, Wq, Wk, Wv, Wo):
        import jax, jax.numpy as jnp
        import numpy as np
        H = 32
        HKV = 8
        D = 1024
        HD = D // H
        S = 256
        MASK_OUT = 0.9
        MIN_REMAIN = 128
        THETA = 10000.0

        def rope_tables(seq_len, hd):
            inv_freq = 1.0 / THETA ** (jnp.arange(0, hd, 2, dtype=jnp.float32) / hd)
            t = jnp.arange(seq_len, dtype=jnp.float32)
            freqs = jnp.outer(t, inv_freq)
            emb = jnp.concatenate([freqs, freqs], axis=-1)
            return (jnp.cos(emb), jnp.sin(emb))

        def rotate_half(x):
            x1, x2 = jnp.split(x, 2, axis=-1)
            return jnp.concatenate([-x2, x1], axis=-1)

        def apply_rope(x, cos, sin):
            return x * cos + rotate_half(x) * sin
        B, Sq, Dm = hidden_states.shape
        dtype = hidden_states.dtype
        neg = jnp.finfo(dtype).min
        q = (hidden_states @ Wq.T).reshape(B, Sq, H, HD).transpose(0, 2, 1, 3)
        k = (hidden_states @ Wk.T).reshape(B, Sq, HKV, HD).transpose(0, 2, 1, 3)
        v = (hidden_states @ Wv.T).reshape(B, Sq, HKV, HD).transpose(0, 2, 1, 3)
        rep = H // HKV
        k = jnp.repeat(k, rep, axis=1)
        v = jnp.repeat(v, rep, axis=1)
        cos, sin = rope_tables(Sq, HD)
        qr = apply_rope(q, cos, sin)
        kr = apply_rope(k, cos, sin)
        draft = jnp.einsum('bhqd,bhkd->bhqk', qr, kr)
        qi = jnp.arange(Sq)
        ki = jnp.arange(Sq)
        causal_future = qi[:, None] < ki[None, :]
        draft = draft + jnp.where(causal_future, neg, jnp.asarray(0.0, dtype))
        num_remain = max(min(Sq, MIN_REMAIN), Sq - int(Sq * MASK_OUT))
        _, draft_indices = jax.lax.top_k(draft, num_remain)
        mask = jnp.full((B, H, Sq, Sq), neg, dtype)
        b_idx = jnp.arange(B)[:, None, None, None]
        h_idx = jnp.arange(H)[None, :, None, None]
        s_idx = jnp.arange(Sq)[None, None, :, None]
        mask = mask.at[b_idx, h_idx, s_idx, draft_indices].set(0.0)
        mask = jnp.where(causal_future[None, None, :, :], neg, mask)
        scores = jnp.einsum('bhqd,bhkd->bhqk', qr, kr) / np.sqrt(HD).astype(np.float32) + mask
        attn = jax.nn.softmax(scores, axis=-1)
        out = jnp.einsum('bhqk,bhkd->bhqd', attn, v)
        out = out.transpose(0, 2, 1, 3).reshape(B, Sq, Dm)
        return out @ Wo.T

    def _L0_ffn_ref(hidden_states, router_weight, router_bias, expert_bias):
        import jax, jax.numpy as jnp
        import numpy as np
        K_TOP = 8
        B, S, H = hidden_states.shape
        E = router_weight.shape[0]
        T = B * S
        flat = hidden_states.reshape(T, H)
        logits = jnp.einsum('th,eh->te', flat, router_weight) + router_bias
        scores = jax.nn.softmax(logits, axis=-1)
        topk_w, topk_idx = jax.lax.top_k(scores, K_TOP)
        w_sum = topk_w.sum(axis=-1, keepdims=True)
        w_dense = jnp.zeros((T, E), dtype=scores.dtype).at[jnp.arange(T)[:, None], topk_idx].add(topk_w)
        bias_mix = jnp.einsum('te,eh->th', w_dense, expert_bias)
        out = flat * w_sum + bias_mix
        return out.reshape(B, S, H)
    x = L0_attn_hidden_states
    x = x + 0.5 * _L0_ffn_ref(_layernorm(x, axis=-1), L0_ffn_router_weight, L0_ffn_router_bias, L0_ffn_expert_bias)
    x = x + _L0_attn_ref(_layernorm(x, axis=-1), L0_attn_Wq, L0_attn_Wk, L0_attn_Wv, L0_attn_Wo)
    x = x + 0.5 * _L0_ffn_ref(_layernorm(x, axis=-1), L0_ffn_router_weight, L0_ffn_router_bias, L0_ffn_expert_bias)
    return x

_drawn_inputs = setup_inputs


def setup_inputs(seed=0):
    import zlib

    import numpy as np

    out = dict(_drawn_inputs(seed))
    spreads = {'L0_ffn_router_bias': (0.0, 0.8)}
    factors = {'L0_attn_Wq': 2.863, 'L0_attn_Wk': 2.668}
    for name, (base, spread) in spreads.items():
        noise = np.random.default_rng([zlib.crc32(name.encode()), seed]).standard_normal(out[name].shape)
        drawn = base * np.exp(spread * noise) if base else spread * noise
        out[name] = jnp.asarray(drawn.astype(out[name].dtype))
    for name, factor in factors.items():
        out[name] = (out[name] * factor).astype(out[name].dtype)
    return out
```

```python
from contextlib import ExitStack
import math

import numpy as np

import concourse.bass as bass
from concourse import mybir

ALU = mybir.AluOpType
ACT = mybir.ActivationFunctionType
AX = mybir.AxisListType
F32 = mybir.dt.float32
BF16 = mybir.dt.bfloat16
I32 = mybir.dt.int32

P = 128
S, D = 2048, 1024
H, HKV, HD = 32, 8, 32
REP = H // HKV
E, TOP = 64, 8
KEEP = max(min(S, 128), S - int(S * 0.9))
THETA = 10000.0
EPS = 1e-5
SCALE = float(np.float32(1.0) / np.sqrt(np.float32(HD)))
TILES = S // P
DC = D // P
QK = (H + HKV) * HD
QKC = QK // P
QKV = QK + HKV * HD
VW = HD + 1
BANK = 512
MASKED = -2.0 ** 124
OPEN = -2.0 ** 123
WINDOW = 7
(TAB_Z, TAB_SLOPE, TAB_K, TAB_COUNT, TAB_OPEN, TAB_INVN, TABS) = range(7)
ORDER = list(range(1, TILES, 2)) + list(range(TILES - 2, -1, -2))
U = 2


def normal_point(p):
    lo, hi = -8.0, 8.0
    for _ in range(60):
        z = (lo + hi) / 2
        lo, hi = (z, hi) if 0.5 * (1 + math.erf(z / math.sqrt(2))) < p else (lo, z)
    return z


def shape_constants():
    inv = (np.float32(1.0) / np.float32(THETA) ** (np.arange(0, HD, 2, dtype=np.float32) / np.float32(HD)))
    angle = np.outer(np.arange(S, dtype=np.float32), inv.astype(np.float32)).astype(np.float32)
    angle = np.concatenate([angle, angle], -1)
    cos, sin = np.cos(angle), np.sin(angle)
    sin[:, :HD // 2] *= -1
    rope = np.concatenate([cos, sin], -1).astype(np.float32)
    tab = np.zeros((S, TABS), np.float32)
    for r in range(S):
        n, width = r + 1, P * (r // P + 1)
        k = min(KEEP, n)
        tab[r, TAB_K] = k
        tab[r, TAB_COUNT] = width / 2 - k
        tab[r, TAB_INVN] = 1.0 / width
        if n > KEEP - 1 and n >= KEEP:
            z = normal_point(1 - min(KEEP / (n + 0.5), 0.998))
            tab[r, TAB_Z] = z
            tab[r, TAB_SLOPE] = math.sqrt(2 * math.pi) * math.exp(z * z / 2) / n
        else:
            tab[r, TAB_OPEN] = OPEN
    eye = np.eye(P, dtype=np.float32)
    future = np.triu(np.full((P, P), MASKED, np.float32), 1)
    steps = np.tile(np.concatenate([np.tile(np.arange(8), REP), np.tile(np.arange(1, 9), REP)]), (P, 1)).astype(np.float32)
    return {"rope": rope, "tab": tab, "eye": eye, "future": future, "steps": steps}


def ffn_vector(nc, dve, link, t, sm, b):
    for j in range(2):
        nc.vector.bn_stats(b.stats[:, t, j * 6:j * 6 + 6], b.x[:, t, j * BANK:(j + 1) * BANK]).then_inc(sm["bn"], 1)
    yield
    dve.wait_ge(sm["bn"], 2 * t + 2)
    nc.vector.bn_aggr(b.mv[:, t, :], b.stats[:, t, :]).then_inc(sm["var"], 1)
    yield
    dve.wait_ge(sm["rstd"], t + 1)
    nc.vector.tensor_scalar(b.xn[:, t, :], b.x[:, t, :], b.mv[:, t, 0:1], b.rstd[:, t, 0:1],
                            ALU.subtract, ALU.mult).then_inc(sm["xn"], 1)
    yield
    dve.wait_ge(sm["logits"], t + 1)
    link(nc.vector.max(b.top[:, t, :], b.psum[:, 4 * t + 2, 0:E]))
    nc.vector.tensor_scalar(b.small[:, t, 0:1], b.top[:, t, 0:1], -1.0, None, ALU.mult).then_inc(sm["negmax"], 1)
    yield
    dve.wait_ge(sm["expd"], t + 1)
    link(nc.vector.max(b.top[:, t, :], b.e64[:, t, :]))
    nc.vector.match_replace(b.rest[:, t, :], b.top[:, t, :], b.e64[:, t, :], 0.0)
    nc.vector.tensor_reduce(b.small[:, t, 2:3], b.top[:, t, :], AX.X, ALU.add)
    link(nc.vector.reciprocal(b.small[:, t, 3:4], b.small[:, t, 1:2]))
    link(nc.vector.tensor_scalar(b.small[:, t, 4:5], b.small[:, t, 3:4], 0.5, None, ALU.mult))
    link(nc.vector.tensor_tensor(b.rest[:, t, :], b.e64[:, t, :], b.rest[:, t, :], ALU.subtract))
    nc.vector.tensor_scalar(b.mix[:, t, :], b.rest[:, t, :], b.small[:, t, 4:5], None, ALU.mult).then_inc(sm["mix"], 1)
    link(nc.vector.tensor_tensor(b.small[:, t, 5:6], b.small[:, t, 2:3], b.small[:, t, 4:5], ALU.mult))
    link(nc.vector.scalar_tensor_tensor(b.x[:, t, :], b.xn[:, t, :], b.small[:, t, 5:6], b.x[:, t, :], ALU.mult, ALU.add))
    yield
    dve.wait_ge(sm["mixed"], t + 1)
    nc.vector.tensor_tensor(b.x[:, t, :], b.x[:, t, :], bank2(b.psum, 4 * t), ALU.add).then_inc(sm["x1"], 1)
    yield


def bank2(psum, first, width=2 * BANK):
    return psum[:, first:first + 4, :].rearrange("p b n -> p (b n)")[:, 0:width]


def ffn_tensor(nc, pe, t, sm, b):
    transpose8(nc, pe, t, sm["xn"], t + 1, b, 4 * t, sm["xT"])
    yield
    pe.wait_ge(sm["xTcopy"], 2 * t + 2)
    logits = b.psum[:, 4 * t + 2, 0:E]
    for c in range(DC):
        nc.tensor.matmul(logits, b.xT[:, t, c, :], b.router[:, c, :], start=(c == 0), stop=False)
    nc.tensor.matmul(logits, b.ones[0:1, :], b.rbias[0:1, :], start=False, stop=True).then_inc(sm["logits"], 1)
    yield
    pe.wait_ge(sm["mix"], t + 1)
    nc.tensor.transpose(b.psum[0:E, 4 * t + 3, 0:P], b.mix[:, t, :], b.eye[:, :]).then_inc(sm["mixT"], 1)
    yield
    pe.wait_ge(sm["mixTcopy"], t + 1)
    for j in range(2):
        last = nc.tensor.matmul(b.psum[:, 4 * t + j, :], b.mixT[:, t, :], b.ebias[:, j * BANK:(j + 1) * BANK],
                                start=True, stop=True)
    last.then_inc(sm["mixed"], 1)
    yield


def transpose8(nc, pe, t, ready, count, b, bank, done):
    pe.wait_ge(ready, count)
    for c in range(DC):
        last = nc.tensor.transpose(b.psum[:, bank + c // 4, (c % 4) * P:(c % 4 + 1) * P],
                                   b.xn[:, t, c * P:(c + 1) * P], b.eye[:, :])
    last.then_inc(done, 1)


def ffn_scalar(nc, act, t, sm, b):
    act.wait_ge(sm["xT"], t + 1)
    copy_xT(nc, t, b, 4 * t, sm["xTcopy"])
    yield
    act.wait_ge(sm["negmax"], t + 1)
    nc.scalar.activation(b.e64[:, t, :], b.psum[:, 4 * t + 2, 0:E], ACT.Exp, bias=b.small[:, t, 0:1],
                         accum_out=b.small[:, t, 1:2]).then_inc(sm["expd"], 1)
    yield
    act.wait_ge(sm["mixT"], t + 1)
    nc.scalar.activation(b.mixT[:, t, :], b.psum[0:E, 4 * t + 3, 0:P], ACT.Copy).then_inc(sm["mixTcopy"], 1)
    yield


def copy_xT(nc, t, b, bank, done):
    for j in range(2):
        nc.scalar.activation(b.xT[:, t, 4 * j:4 * j + 4, :].rearrange("p c n -> p (c n)"),
                             b.psum[:, bank + j, :], ACT.Copy).then_inc(done, 1)


def rstd_pool(nc, pool, t, var, count, done, b):
    plink = b.plink
    pool.wait_ge(var, count)
    v, r, a = b.pw[:, t, 0:1], b.pw[:, t, 1:2], b.pw[:, t, 2:3]
    plink(nc.gpsimd.tensor_scalar(v, b.mv[:, t, 1:2], EPS, None, ALU.add))
    plink(nc.gpsimd.tensor_tensor(r, v, b.mhalf[:, 0:1], ALU.pow))
    plink(nc.gpsimd.tensor_tensor(a, r, r, ALU.mult))
    plink(nc.gpsimd.tensor_tensor(a, a, v, ALU.mult))
    plink(nc.gpsimd.tensor_scalar(a, a, -0.5, 1.5, ALU.mult, ALU.add))
    nc.gpsimd.tensor_tensor(b.rstd[:, t, 0:1], r, a, ALU.mult).then_inc(done, 1)


def interleave(parts):
    parts = list(parts)
    while parts:
        parts = [p for p in parts if next(p, "end") != "end"]


class Names:
    pass


def semaphores(nc, ctx, names, prefix):
    return {n: ctx.enter_context(nc.semaphore(f"{prefix}_{n}")) for n in names.split()}


def clear(nc, sems):
    nc.all_engine_barrier()
    for s in sems:
        nc.gpsimd.sem_clear(s)
    nc.all_engine_barrier()


def linker(engine, sem):
    count = [0]

    def link(ins):
        count[0] += 1
        ins.then_inc(sem, 1)
        engine.wait_ge(sem, count[0])
    return link


def ffn_buffers(nc, ctx, b, phase):
    sb = lambda n, s, d=F32: ctx.enter_context(nc.sbuf_tensor(f"{phase}_{n}", s, d))
    b.x = sb("x", [P, U, D])
    b.xn = sb("xn", [P, U, D])
    b.xT = sb("xT", [P, U, DC, P])
    b.stats = sb("stats", [P, U, 12])
    b.mv = sb("mv", [P, U, 2])
    b.rstd = sb("rstd", [P, U, 1])
    b.pw = sb("pw", [P, U, 4])
    b.small = sb("small", [P, U, 8])
    b.top = sb("top", [P, U, TOP])
    b.e64 = sb("e64", [P, U, E])
    b.rest = sb("rest", [P, U, E])
    b.mix = sb("mix", [P, U, E])
    b.mixT = sb("mixT", [E, U, P])


FFN_SEMS = "x bn var rstd xn xT xTcopy logits negmax expd mix mixT mixTcopy mixed x1 vchain pchain out "


def phase_a(nc, b, x_dram, dram):
    with ExitStack() as ctx:
        sb = lambda n, s, d=F32: ctx.enter_context(nc.sbuf_tensor(n, s, d))
        ffn_buffers(nc, ctx, b, "a")
        wqkv = sb("wqkv", [P, DC, QKV])
        rope = sb("rope", [P, U, 2 * HD])
        tab = sb("tab_a", [P, U, TABS])
        rot = sb("rot", [P, U, H + HKV, HD])
        qk = sb("qk", [P, U, H + HKV, HD])
        qkT = sb("qkT", [P, U, QKC, P])
        krep = sb("krep", [P, U, HKV, REP, HD])
        k1 = sb("k1", [P, U, HKV, VW])
        moments = sb("moments", [P, U, HKV, VW])
        prod = sb("prod", [P, U, H, HD])
        sums = sb("sums", [P, U, 2, H])
        gs = sb("gs", [P, U, 4, H])
        half = sb("half", [P, H])

        su = semaphores(nc, ctx, "w fill", "sa")
        with nc.Block() as block:
            @block.sync
            def _(sp):
                sp.dma_start(wqkv[:, :, :], dram["wqkv"].rearrange("(c p) n -> p c n", p=P)).then_inc(su["w"], 16)
                sp.dma_start(b.router[:, :, :], dram["router"].rearrange("(c p) e -> p c e", p=P)).then_inc(su["w"], 16)
                sp.dma_start(b.ebias[:, :], dram["ebias"]).then_inc(su["w"], 16)
                sp.dma_start(b.rbias[:, :], dram["rbias"]).then_inc(su["w"], 16)
                sp.dma_start(b.eye[:, :], dram["eye"]).then_inc(su["w"], 16)
                sp.dma_start(b.future[:, :], dram["future"]).then_inc(su["w"], 16)
                sp.dma_start(b.steps[:, :], dram["steps"]).then_inc(su["w"], 16)
                sp.dma_start(b.tab[:, :, :], dram["tab"].rearrange("(t p) c -> p t c", p=P)).then_inc(su["w"], 16)
                sp.wait_ge(su["w"], 8 * 16)

            @block.vector
            def _(dve):
                nc.vector.memset(b.ones[:, :], 1.0)
                nc.vector.memset(b.mhalf[:, :], -0.5)
                nc.vector.memset(b.minus[:, :], -1.0)
                nc.vector.memset(half[:, :], 0.5)
                nc.vector.memset(moments[:, :, :, :], 0.0)
                nc.vector.memset(b.v_all[:, :, :, :], 1.0)
                nc.vector.memset(k1[:, :, :, :], 1.0).then_inc(su["fill"], 1)

        with nc.Fori(0, TILES // U) as it, ExitStack() as ctx2:
            sm = semaphores(nc, ctx2, FFN_SEMS + "tabs x1out var2 rstd2 h hT hTcopy qkv cosd sind vcopy rot qkT "
                            "qkTcopy kk mom momsum y prod sums guess", "a")
            loaded = [ctx2.enter_context(nc.semaphore(f"a_load{t}")) for t in range(U)]
            with nc.Block() as block:
                @block.sync
                def _(sp):
                    for t in range(U):
                        rows = bass.ds((it * U + t) * P, P)
                        sp.dma_start(b.x[:, t, :], x_dram[rows, :]).then_inc(loaded[t], 16)
                        sp.dma_start(rope[:, t, :], dram["rope"][rows, :]).then_inc(loaded[t], 16)
                        sp.dma_start(tab[:, t, :], dram["tab"][rows, :]).then_inc(loaded[t], 16)
                    for t in range(U):
                        rows = bass.ds((it * U + t) * P, P)
                        sp.wait_ge(sm["x1"], t + 1)
                        sp.dma_start(dram["x1"][rows, :], b.x[:, t, :]).then_inc(sm["x1out"], 16)
                    for t in range(U):
                        rows = bass.ds((it * U + t) * P, P)
                        sp.wait_ge(sm["qkTcopy"], 3 * t + 3)
                        sp.dma_start(dram["qkT"].rearrange("(c p) s -> p c s", p=P)[:, :, rows],
                                     qkT[:, t, :, :]).then_inc(sm["out"], 16)
                    sp.wait_ge(sm["x1out"], 16 * U)
                    sp.wait_ge(sm["out"], 16 * U)

                @block.tensor
                def _(pe):
                    def tile(t):
                        yield from ffn_tensor(nc, pe, t, sm, b)
                        transpose8(nc, pe, t, sm["h"], t + 1, b, 4 * t + 2, sm["hT"])
                        yield
                        pe.wait_ge(sm["hTcopy"], 2 * t + 2)
                        pe.wait_ge(sm["x1"], t + 1)
                        for c in range(DC):
                            for j in range(QKV // BANK):
                                last = nc.tensor.matmul(b.psum[:, 4 * t + j, :], b.xT[:, t, c, :],
                                                        wqkv[:, c, j * BANK:(j + 1) * BANK],
                                                        start=(c == 0), stop=(c == DC - 1))
                        last.then_inc(sm["qkv"], 1)
                        yield
                        pe.wait_ge(sm["rot"], t + 1)
                        pe.wait_ge(sm["vcopy"], t + 1)
                        for c in range(QKC):
                            last = nc.tensor.transpose(
                                b.psum[:, 4 * t + c // 4, (c % 4) * P:(c % 4 + 1) * P],
                                qk[:, t, 4 * c:4 * c + 4, :].rearrange("p h d -> p (h d)"), b.eye[:, :])
                        last.then_inc(sm["qkT"], 1)
                        yield
                        pe.wait_ge(sm["kk"], t + 1)
                        for g in range(HKV):
                            last = nc.tensor.matmul(b.psum[:, 4 * t + 3, g * VW:(g + 1) * VW],
                                                    krep[:, t, g, :, :].rearrange("p r d -> p (r d)"),
                                                    k1[:, t, g, :], start=True, stop=True)
                        last.then_inc(sm["mom"], 1)
                        yield
                        pe.wait_ge(sm["momsum"], t + 1)
                        pe.wait_ge(sm["qkTcopy"], 3 * t + 3)
                        for g in range(HKV):
                            for r in range(REP):
                                q = slice(r * HD, (r + 1) * HD)
                                last = nc.tensor.matmul(b.psum[:, 4 * t + r, g * VW:(g + 1) * VW], qkT[q, t, g, :],
                                                        moments[q, t, g, :], start=True, stop=True)
                        last.then_inc(sm["y"], 1)
                        yield
                    interleave(tile(t) for t in range(U))

                @block.scalar
                def _(act):
                    def tile(t):
                        yield from ffn_scalar(nc, act, t, sm, b)
                        act.wait_ge(sm["hT"], t + 1)
                        act.wait_ge(sm["logits"], t + 1)
                        copy_xT(nc, t, b, 4 * t + 2, sm["hTcopy"])
                        yield
                        act.wait_ge(sm["qkv"], t + 1)
                        act.wait_ge(sm["sind"], 3 * t + 3)
                        nc.scalar.activation(b.v_all[:, it * U + t, :, 0:HD],
                                             b.psum[:, 4 * t + 2, 256:512].rearrange("p (g d) -> p g d", g=HKV),
                                             ACT.Copy).then_inc(sm["vcopy"], 1)
                        yield
                        act.wait_ge(sm["qkT"], t + 1)
                        for j, c in enumerate((0, 4, 8)):
                            w = min(4, QKC - c)
                            nc.scalar.activation(qkT[:, t, c:c + w, :].rearrange("p c n -> p (c n)"),
                                                 b.psum[:, 4 * t + j, 0:w * P], ACT.Copy).then_inc(sm["qkTcopy"], 1)
                        yield
                    interleave(tile(t) for t in range(U))

                @block.gpsimd
                def _(pool):
                    b.plink = plink = linker(pool, sm["pchain"])

                    def tile(t):
                        rstd_pool(nc, pool, t, sm["var"], t + 1, sm["rstd"], b)
                        yield
                        pool.wait_ge(sm["xn"], t + 1)
                        rstd_pool(nc, pool, t, sm["var2"], t + 1, sm["rstd2"], b)
                        yield
                        pool.wait_ge(sm["sind"], 3 * t + 3)
                        nc.gpsimd.tensor_tensor(qk[:, t, :, :], qk[:, t, :, :], rot[:, t, :, :],
                                                ALU.add).then_inc(sm["rot"], 1)
                        pool.wait_ge(sm["rot"], t + 1)
                        for r in range(REP):
                            nc.gpsimd.tensor_copy(krep[:, t, :, r, :], qk[:, t, H:, :])
                        nc.gpsimd.tensor_copy(k1[:, t, :, 0:HD], qk[:, t, H:, :]).then_inc(sm["kk"], 1)
                        yield
                        pool.wait_ge(sm["sums"], 2 * t + 2)
                        pool.wait_ge(loaded[t], 48)
                        e2, s1 = sums[:, t, 0, :], sums[:, t, 1, :]
                        mean, sq, t0, sl = (gs[:, t, j, :] for j in range(4))
                        col = lambda c: tab[:, t, c:c + 1]
                        plink(nc.gpsimd.tensor_scalar(mean, s1, col(TAB_INVN), None, ALU.mult))
                        plink(nc.gpsimd.tensor_tensor(sq, mean, mean, ALU.mult))
                        plink(nc.gpsimd.tensor_scalar(t0, e2, col(TAB_INVN), None, ALU.mult))
                        plink(nc.gpsimd.tensor_tensor(t0, t0, sq, ALU.subtract))
                        plink(nc.gpsimd.tensor_scalar(t0, t0, 1e-30, None, ALU.max))
                        plink(nc.gpsimd.tensor_tensor(sq, t0, half[:, :], ALU.pow))
                        plink(nc.gpsimd.tensor_scalar(t0, sq, col(TAB_Z), None, ALU.mult))
                        plink(nc.gpsimd.tensor_tensor(t0, t0, mean, ALU.add))
                        plink(nc.gpsimd.tensor_scalar(t0, t0, col(TAB_OPEN), None, ALU.add))
                        plink(nc.gpsimd.tensor_scalar(sl, sq, col(TAB_SLOPE), None, ALU.mult))
                        nc.gpsimd.tensor_copy(b.t_all[:, it * U + t, :], t0)
                        nc.gpsimd.tensor_copy(b.slope_all[:, it * U + t, :], sl).then_inc(sm["guess"], 1)
                        yield
                    interleave(tile(t) for t in range(U))

                @block.vector
                def _(dve):
                    link = linker(dve, sm["vchain"])

                    def tile(t):
                        dve.wait_ge(loaded[t], 48)
                        yield from ffn_vector(nc, dve, link, t, sm, b)
                        dve.wait_ge(sm["x1"], t + 1)
                        for j in range(2):
                            last = nc.vector.bn_stats(b.stats[:, t, j * 6:j * 6 + 6],
                                                      b.x[:, t, j * BANK:(j + 1) * BANK])
                            if j:
                                link(last)
                        nc.vector.bn_aggr(b.mv[:, t, :], b.stats[:, t, :]).then_inc(sm["var2"], 1)
                        yield
                        dve.wait_ge(sm["rstd2"], t + 1)
                        dve.wait_ge(sm["xT"], t + 1)
                        nc.vector.tensor_scalar(b.xn[:, t, :], b.x[:, t, :], b.mv[:, t, 0:1], b.rstd[:, t, 0:1],
                                                ALU.subtract, ALU.mult).then_inc(sm["h"], 1)
                        yield
                        dve.wait_ge(sm["qkv"], t + 1)
                        proj = bank2(b.psum, 4 * t, QK).rearrange("p (h d) -> p h d", d=HD)
                        lo, hi = slice(0, HD // 2), slice(HD // 2, HD)
                        cos = rope[:, t:t + 1, 0:HD].broadcast_to([P, H + HKV, HD])
                        sin = rope[:, t:t + 1, HD:2 * HD]
                        nc.vector.tensor_tensor(qk[:, t, :, :], proj, cos, ALU.mult).then_inc(sm["sind"], 1)
                        nc.vector.tensor_tensor(rot[:, t, :, lo], proj[:, :, hi],
                                                sin[:, :, lo].broadcast_to([P, H + HKV, HD // 2]),
                                                ALU.mult).then_inc(sm["sind"], 1)
                        nc.vector.tensor_tensor(rot[:, t, :, hi], proj[:, :, lo],
                                                sin[:, :, hi].broadcast_to([P, H + HKV, HD // 2]),
                                                ALU.mult).then_inc(sm["sind"], 1)
                        yield
                        dve.wait_ge(sm["mom"], t + 1)
                        if t:
                            dve.wait_ge(sm["momsum"], t)
                        nc.vector.tensor_tensor(moments[:, t, :, :], moments[:, 1 - t, :, :],
                                                b.psum[:, 4 * t + 3, 0:HKV * VW].rearrange("p (g d) -> p g d", g=HKV),
                                                ALU.add).then_inc(sm["momsum"], 1)
                        yield
                        dve.wait_ge(sm["y"], t + 1)
                        for r in range(REP):
                            y = b.psum[:, 4 * t + r, 0:HKV * VW].rearrange("p (g d) -> p g d", g=HKV)
                            copied = nc.vector.tensor_copy(sums[:, t, 1, r::REP], y[:, :, HD])
                            last = nc.vector.tensor_tensor(prod[:, t, r::REP, :], y[:, :, 0:HD], qk[:, t, r:H:REP, :],
                                                           ALU.mult)
                        copied.then_inc(sm["sums"], 1)
                        link(last)
                        nc.vector.tensor_reduce(sums[:, t, 0, :], prod[:, t, :, :], AX.X, ALU.add).then_inc(sm["sums"], 1)
                        yield
                    interleave(tile(t) for t in range(U))
            clear(nc, [*sm.values(), *loaded])


def phase_c(nc, b, dram, out):
    with ExitStack() as ctx:
        sb = lambda n, s, d=F32: ctx.enter_context(nc.sbuf_tensor(n, s, d))
        ffn_buffers(nc, ctx, b, "c")
        wo = sb("wo", [P, DC, D])
        su = semaphores(nc, ctx, "w", "sc")
        with nc.Block() as block:
            @block.sync
            def _(sp):
                sp.dma_start(wo[:, :, :], dram["wo"].rearrange("(c p) n -> p c n", p=P)).then_inc(su["w"], 16)
                sp.wait_ge(su["w"], 16)

        with nc.Fori(0, TILES // U) as it, ExitStack() as ctx2:
            sm = semaphores(nc, ctx2, FFN_SEMS + "aT aTcopy proj xsum", "c")
            loaded = [ctx2.enter_context(nc.semaphore(f"c_load{t}")) for t in range(U)]
            with nc.Block() as block:
                @block.sync
                def _(sp):
                    for t in range(U):
                        rows = bass.ds((it * U + t) * P, P)
                        sp.dma_start(b.xn[:, t, :], dram["attn"][rows, :]).then_inc(loaded[t], 16)
                        sp.dma_start(b.x[:, t, :], dram["x1"][rows, :]).then_inc(loaded[t], 16)
                    for t in range(U):
                        rows = bass.ds((it * U + t) * P, P)
                        sp.wait_ge(sm["x1"], t + 1)
                        sp.dma_start(out[rows, :], b.x[:, t, :]).then_inc(sm["out"], 16)
                    sp.wait_ge(sm["out"], 16 * U)

                @block.tensor
                def _(pe):
                    def tile(t):
                        transpose8(nc, pe, t, loaded[t], 32, b, 4 * t + 2, sm["aT"])
                        yield
                        pe.wait_ge(sm["aTcopy"], 2 * t + 2)
                        for c in range(DC):
                            for j in range(2):
                                last = nc.tensor.matmul(b.psum[:, 4 * t + j, :], b.xT[:, t, c, :],
                                                        wo[:, c, j * BANK:(j + 1) * BANK],
                                                        start=(c == 0), stop=(c == DC - 1))
                        last.then_inc(sm["proj"], 1)
                        yield
                        yield from ffn_tensor(nc, pe, t, sm, b)
                    interleave(tile(t) for t in range(U))

                @block.scalar
                def _(act):
                    def tile(t):
                        act.wait_ge(sm["aT"], t + 1)
                        copy_xT(nc, t, b, 4 * t + 2, sm["aTcopy"])
                        yield
                        act.wait_ge(sm["proj"], t + 1)
                        yield from ffn_scalar(nc, act, t, sm, b)
                    interleave(tile(t) for t in range(U))

                @block.gpsimd
                def _(pool):
                    b.plink = linker(pool, sm["pchain"])

                    def tile(t):
                        rstd_pool(nc, pool, t, sm["var"], t + 1, sm["rstd"], b)
                        yield
                    interleave(tile(t) for t in range(U))

                @block.vector
                def _(dve):
                    link = linker(dve, sm["vchain"])

                    def tile(t):
                        dve.wait_ge(loaded[t], 32)
                        dve.wait_ge(sm["proj"], t + 1)
                        link(nc.vector.tensor_tensor(b.x[:, t, :], b.x[:, t, :], bank2(b.psum, 4 * t), ALU.add))
                        yield
                        yield from ffn_vector(nc, dve, link, t, sm, b)
                    interleave(tile(t) for t in range(U))
            clear(nc, [*sm.values(), *loaded])


def uses_of_slots():
    return [(p, h, c, min(2 * BANK, P * (i + 1) - 2 * BANK * c))
            for p, i in enumerate(ORDER) for h in range(REP) for c in range(-(-P * (i + 1) // (2 * BANK)))]


def phase_b(nc, b, dram):
    uses = uses_of_slots()
    evacuated = {}
    for n, (p, h, c, w) in enumerate(uses):
        evacuated[p, h] = n + 1
    chunks = [-(-P * (i + 1) // (2 * BANK)) for i in ORDER]
    blocks_before = [sum(ORDER[q] + 1 for q in range(p)) for p in range(TILES + 1)]

    with ExitStack() as ctx:
        sb = lambda n, s, d=F32: ctx.enter_context(nc.sbuf_tensor(n, s, d))
        q_sb = sb("q_sb", [P, S])
        k_sb = sb("k_sb", [P, S])
        v_sb = sb("v_sb", [P, TILES, VW])
        tg = sb("tg", [P, TILES, REP])
        slg = sb("slg", [P, TILES, REP])
        sc = sb("sc", [P, 2, REP, S])
        ex = sb("ex", [P, REP, S])
        keys = sb("keys", [P, 2, S])
        junk = sb("junk", [P, 2, S], BF16)
        pT = sb("pT", [P, 3, REP * P])
        mx = sb("mx", [P, 2, 2, REP])
        nmx = sb("nmx", [P, 2, REP])
        sgn = sb("sgn", [P, 2, 3, REP])
        tt = sb("tt", [P, 2, 4, REP])
        dd = sb("dd", [P, 2, 3, REP])
        pw = sb("pw_b", [P, 8, REP])
        cnt = sb("cnt", [P, REP])
        vs = sb("vs", [P, 12, REP])
        dirn = sb("dirn", [P, REP], I32)
        flip = sb("flip", [P, REP], I32)
        near = sb("near", [P, REP, 8])
        diff = sb("diff", [P, REP, 8])
        pick = sb("pick", [P, 4, REP, 8])
        badf = sb("badf", [1, 1])
        bad1 = sb("bad1", [1, 1], I32)
        rec = sb("rec", [P, 2, REP])
        o_sb = sb("o_sb", [P, 2, REP, HD])
        fb = sb("fb", [P, 16])
        fbi = sb("fbi", [P, 8], I32)
        psum = b.psum

        def slot(n):
            return bank2(psum, 2 * (n % 2))

        def widths(p):
            return P * (ORDER[p] + 1)

        with nc.Fori(0, HKV) as g, ExitStack() as ctx2:
            sm = semaphores(nc, ctx2, "q k vt s evac nmx c1 c2 c3 t1 t2 t3 expd act vchain pchain thr prob pT pTcopy pv "
                            "bad badsum norm junk", "b")
            written = [ctx2.enter_context(nc.semaphore(f"b_written{n}")) for n in range(2)]
            with nc.Block() as block:
                @block.sync
                def _(sp):
                    sp.dma_start(q_sb[:, :], dram["qkT"][bass.ds(g * P, P), :]).then_inc(sm["q"], 16)
                    for r in range(REP):
                        sp.dma_start(k_sb[r * HD:(r + 1) * HD, :],
                                     dram["qkT"][bass.ds(g * HD + H * HD, HD), :]).then_inc(sm["k"], 16)
                    for p, i in enumerate(ORDER):
                        sp.wait_ge(sm["norm"], p + 1)
                        sp.dma_start(dram["attn"][i * P:(i + 1) * P, bass.ds(g * P, P)],
                                     o_sb[:, p % 2, :, :].rearrange("p h d -> p (h d)")).then_inc(written[p % 2], 16)
                    for w in written:
                        sp.wait_ge(w, 16 * TILES // 2)

                @block.tensor
                def _(pe):
                    pe.wait_ge(sm["q"], 16)
                    pe.wait_ge(sm["k"], 64)
                    pe.wait_ge(sm["vt"], 3)

                    def scores(p):
                        i = ORDER[p]
                        for n, (pp, h, c, w) in enumerate(uses):
                            if pp != p:
                                continue
                            if n >= 2:
                                pe.wait_ge(sm["evac"], n - 1)
                            q = slice(h * HD, (h + 1) * HD)
                            for j in range(0, w, BANK):
                                wj = min(BANK, w - j)
                                col = c * 2 * BANK + j
                                diag = col + wj == P * (i + 1)
                                last = nc.tensor.matmul(slot(n)[:, j:j + wj], q_sb[q, i * P:(i + 1) * P],
                                                        k_sb[q, col:col + wj], start=True, stop=not diag)
                                if diag:
                                    last = nc.tensor.matmul(slot(n)[:, j + wj - P:j + wj], b.eye[:, :],
                                                            b.future[:, :], start=False, stop=True)
                            last.then_inc(sm["s"], 1)

                    def flags(p):
                        pe.wait_ge(sm["bad"], p + 1)
                        if p >= 2:
                            pe.wait_ge(sm["norm"], p - 1)
                        nc.tensor.matmul(psum[0:1, 6 + p % 2, 256:256 + REP], b.ones[:, 0:1], vs[:, 11, :],
                                         start=True, stop=True).then_inc(sm["badsum"], 1)

                    def values(p):
                        pe.wait_ge(sm["prob"], REP * p + REP)
                        nb = ORDER[p] + 1

                        def turn(kb):
                            n = blocks_before[p] + kb
                            if n >= 2:
                                pe.wait_ge(sm["pTcopy"], n - 1)
                            for h in range(REP):
                                last = nc.tensor.transpose(psum[:, 4 + n % 2, h * P:(h + 1) * P],
                                                           ex[:, h, kb * P:(kb + 1) * P], b.eye[:, :])
                            last.then_inc(sm["pT"], 1)

                        def product(kb):
                            n = blocks_before[p] + kb
                            pe.wait_ge(sm["pTcopy"], n + 1)
                            for h in range(REP):
                                last = nc.tensor.matmul(psum[:, 6 + p % 2, h * VW:(h + 1) * VW],
                                                        pT[:, n % 3, h * P:(h + 1) * P], v_sb[:, kb, :],
                                                        start=(kb == 0 and h == 0), stop=(kb == nb - 1),
                                                        skip_group_check=True)
                            last.then_inc(sm["pv"], 1)

                        for kb in range(nb):
                            turn(kb)
                            if kb:
                                product(kb - 1)
                        product(nb - 1)

                    for p in range(TILES + 1):
                        if p < TILES:
                            scores(p)
                        if p:
                            if ORDER[p - 1]:
                                flags(p - 1)
                            values(p - 1)

                @block.scalar
                def _(act):
                    signs = [0]

                    def count(p, h, k, t, done):
                        n = signs[0]
                        signs[0] += 1
                        if n >= 2:
                            act.wait_ge(sm["junk"], n - 1)
                        w = widths(p)
                        nc.scalar.activation(junk[:, n % 2, 0:w], sc[:, p % 2, h, 0:w], ACT.Sign, bias=t, scale=-1.0,
                                             accum_out=sgn[:, p % 2, k, h:h + 1]).then_inc(sm["junk"], 1)
                        return n

                    def exponentials(p, heads):
                        act.wait_ge(sm["nmx"], p + 1)
                        for h in heads:
                            if p:
                                act.wait_ge(sm["pT"], blocks_before[p])
                            w = widths(p)
                            nc.scalar.activation(ex[:, h, 0:w], sc[:, p % 2, h, 0:w], ACT.Exp,
                                                 bias=nmx[:, p % 2, h:h + 1], scale=SCALE).then_inc(sm["expd"], 1)

                    for p in range(TILES + 1):
                        if p < TILES and ORDER[p]:
                            for h in range(REP):
                                act.wait_ge(sm["evac"], evacuated[p, h])
                                if h == 0:
                                    act.wait_ge(sm["vt"], 3)
                                count(p, h, 0, tg[:, ORDER[p], h:h + 1], None)
                        if p:
                            exponentials(p - 1, (0, 1))
                        if p < TILES and ORDER[p]:
                            act.wait_ge(sm["t1"], p + 1)
                            for h in range(REP):
                                count(p, h, 1, tt[:, p % 2, 0, h:h + 1], None)
                        if p:
                            exponentials(p - 1, (2, 3))
                        if p < TILES and ORDER[p]:
                            act.wait_ge(sm["t2"], p + 1)
                            for h in range(REP):
                                count(p, h, 2, tt[:, p % 2, 1, h:h + 1], None)
                        if p:
                            for kb in range(ORDER[p - 1] + 1):
                                n = blocks_before[p - 1] + kb
                                act.wait_ge(sm["pT"], n + 1)
                                if n >= 3:
                                    act.wait_ge(sm["pv"], n - 2)
                                nc.scalar.activation(pT[:, n % 3, :], psum[:, 4 + n % 2, :], ACT.Copy)\
                                    .then_inc(sm["pTcopy"], 1)

                @block.gpsimd
                def _(pool):
                    link = linker(pool, sm["pchain"])
                    nc.gpsimd.tensor_copy(v_sb[:, :, :], b.v_all[:, :, g, :]).then_inc(sm["vt"], 1)
                    nc.gpsimd.tensor_copy(tg[:, :, :], b.t_all[:, :, bass.ds(g * REP, REP)]).then_inc(sm["vt"], 1)
                    nc.gpsimd.tensor_copy(slg[:, :, :], b.slope_all[:, :, bass.ds(g * REP, REP)]).then_inc(sm["vt"], 1)
                    pool.wait_ge(sm["vt"], 3)
                    gp = nc.gpsimd
                    rounds = 0

                    def update(p, k, done):
                        i = ORDER[p]
                        before = tg[:, i, :] if k == 0 else tt[:, p % 2, k - 1, :]
                        d = dd[:, p % 2, k, :]
                        st = slg[:, i, :]
                        gate, move, den, s, lo = (pw[:, j, :] for j in range(5))
                        link(gp.tensor_scalar(d, sgn[:, p % 2, k, :], -0.5, b.tab[:, i, TAB_COUNT:TAB_COUNT + 1],
                                              ALU.mult, ALU.add))
                        link(gp.tensor_tensor(gate, d, d, ALU.mult))
                        link(gp.tensor_scalar(gate, gate, (WINDOW - 0.4) ** 2, None, ALU.is_gt))
                        if k == 0:
                            link(gp.tensor_tensor(move, d, st, ALU.mult))
                        else:
                            older = tg[:, i, :] if k == 1 else tt[:, p % 2, k - 2, :]
                            link(gp.tensor_tensor(den, dd[:, p % 2, k - 1, :], d, ALU.subtract))
                            link(gp.tensor_tensor(s, before, older, ALU.subtract))
                            link(gp.tensor_tensor(s, s, den, ALU.mult))
                            link(gp.tensor_tensor(den, den, den, ALU.mult))
                            link(gp.tensor_scalar(den, den, 0.25, None, ALU.max))
                            link(gp.tensor_scalar(lo, st, 1e-30, None, ALU.max))
                            link(gp.tensor_tensor(den, den, lo, ALU.mult))
                            link(gp.tensor_tensor(den, den, b.minus[:, :], ALU.pow))
                            link(gp.tensor_tensor(s, s, den, ALU.mult))
                            link(gp.tensor_scalar(s, s, 0.5, 2.0, ALU.max, ALU.min))
                            link(gp.tensor_tensor(s, s, st, ALU.mult))
                            link(gp.tensor_tensor(move, d, s, ALU.mult))
                        link(gp.tensor_tensor(move, move, gate, ALU.mult))
                        gp.tensor_tensor(tt[:, p % 2, k, :], before, move, ALU.add).then_inc(done, 1)

                    for p in range(TILES):
                        pool.wait_ge(sm["evac"], evacuated[p, REP - 1])
                        m = mx[:, p % 2, chunks[p] - 1, :]
                        if p >= 2:
                            pool.wait_ge(sm["expd"], REP * (p - 1))
                        gp.tensor_scalar(nmx[:, p % 2, :], m, -SCALE, None, ALU.mult).then_inc(sm["nmx"], 1)
                        if ORDER[p] == 0:
                            continue
                        for k, done in enumerate((sm["t1"], sm["t2"], sm["t3"])):
                            rounds += REP
                            pool.wait_ge(sm["junk"], rounds)
                            if k == 0 and p >= 2:
                                pool.wait_ge(sm["thr"], p - 1)
                            update(p, k, done)

                @block.vector
                def _(dve):
                    link = linker(dve, sm["vchain"])
                    v = nc.vector
                    dve.wait_ge(sm["vt"], 3)

                    def evacuate(p, h):
                        for n, (pp, hh, c, w) in enumerate(uses):
                            if (pp, hh) != (p, h):
                                continue
                            dve.wait_ge(sm["s"], n + 1)
                            if p >= 2 and h == 0 and c == 0:
                                dve.wait_ge(sm["nmx"], p - 1)
                            if c:
                                dve.wait_ge(sm["evac"], n)
                            v.tensor_scalar(sc[:, p % 2, h, c * 2 * BANK:c * 2 * BANK + w], slot(n)[:, 0:w], 0.0,
                                            mx[:, p % 2, 0, h:h + 1] if c else None, ALU.add, ALU.max, accum_out=mx[:, p % 2, c, h:h + 1]).then_inc(sm["evac"], 1)

                    def count(p, h):
                        w = widths(p)
                        link(v.tensor_scalar(keys[:, h % 2, 0:w], sc[:, p % 2, h, 0:w], tt[:, p % 2, 2, h:h + 1], None,
                                             ALU.is_ge, ALU.add, accum_out=cnt[:, h:h + 1]))

                    def select(p):
                        i, w = ORDER[p], widths(p)
                        t3 = tt[:, p % 2, 2, :]
                        d, a, j1, j2, dk, dn, gap, x1, x2, x3, nz, bad = (vs[:, j, :] for j in range(12))
                        kt = b.tab[:, i, TAB_K:TAB_K + 1]
                        link(v.tensor_scalar(d, cnt[:, :], kt, None, ALU.subtract))
                        link(v.tensor_scalar(dirn[:, :], d, 0.0, None, ALU.is_gt))
                        link(v.tensor_scalar(flip[:, :], dirn[:, :], 29, 0x1FFFFFFF, ALU.logical_shift_left,
                                             ALU.bitwise_or))
                        link(v.scalar_tensor_tensor(a, d, -1.0, d, ALU.mult, ALU.max))
                        link(v.tensor_scalar(j1, d, -1.0, -1.0, ALU.mult, ALU.add))
                        link(v.tensor_tensor(j1, j1, d, ALU.max))
                        link(v.scalar_tensor_tensor(j2, a, 2.0, j1, ALU.mult, ALU.subtract))
                        link(v.tensor_scalar(nz, a, 0.0, None, ALU.is_gt))
                        for h in range(REP):
                            z = keys[:, h % 2, 0:w]
                            link(v.tensor_scalar(z, sc[:, p % 2, h, 0:w], t3[:, h:h + 1], None, ALU.subtract))
                            link(v.tensor_scalar(z.bitcast(I32), z.bitcast(I32), 2, flip[:, h:h + 1],
                                                 ALU.logical_shift_right, ALU.bitwise_xor))
                            link(v.max(near[:, h, :], z))
                        wide = lambda x: x.rearrange("p (h o) -> p h o", o=1).broadcast_to([P, REP, 8])
                        zero = b.steps[:, 0:REP * 8].rearrange("p (h o) -> p h o", h=REP)
                        one = b.steps[:, REP * 8:].rearrange("p (h o) -> p h o", h=REP)
                        link(v.tensor_tensor(diff[:, :, :].bitcast(I32), near[:, :, :].bitcast(I32), wide(flip[:, :]),
                                             ALU.bitwise_xor))
                        link(v.tensor_scalar(diff[:, :, :].bitcast(I32), diff[:, :, :].bitcast(I32), 2, None,
                                             ALU.logical_shift_left))
                        link(v.tensor_tensor(pick[:, 0, :, :], zero, wide(j1), ALU.is_equal))
                        link(v.tensor_tensor(pick[:, 1, :, :], one, wide(j2), ALU.is_equal))
                        link(v.tensor_tensor(pick[:, 0, :, :], pick[:, 0, :, :], diff[:, :, :], ALU.mult))
                        link(v.tensor_tensor(pick[:, 1, :, :], pick[:, 1, :, :], diff[:, :, :], ALU.mult))
                        link(v.tensor_reduce(dk, pick[:, 0, :, :], AX.X, ALU.add))
                        link(v.tensor_reduce(dn, pick[:, 1, :, :], AX.X, ALU.add))
                        link(v.tensor_tensor(gap, dk, dn, ALU.subtract))
                        link(v.scalar_tensor_tensor(x1, dk, -1.0, dk, ALU.mult, ALU.max))
                        link(v.scalar_tensor_tensor(x2, gap, 2.0 ** 19, x1, ALU.mult, ALU.is_le))
                        link(v.tensor_tensor(x2, x2, nz, ALU.mult))
                        if p:
                            dve.wait_ge(sm["badsum"], sum(1 for q in range(p) if ORDER[q]))
                        link(v.scalar_tensor_tensor(bad, a, WINDOW + 0.5, x2, ALU.is_gt, ALU.max))
                        link(v.scalar_tensor_tensor(x3, gap, -0.25, dk, ALU.mult, ALU.add))
                        link(v.tensor_tensor(x3, x3, nz, ALU.mult))
                        v.tensor_tensor(tt[:, p % 2, 3, :], t3, x3, ALU.add).then_inc(sm["bad"], 1)

                    def fall_back(p):
                        i, w = ORDER[p], widths(p)
                        kt = b.tab[:, i, TAB_K:TAB_K + 1]
                        dve.wait_ge(sm["badsum"], sum(1 for q in range(p + 1) if ORDER[q]))
                        dve.wait_ge(sm["bad"], sum(1 for q in range(p + 1) if ORDER[q]))
                        link(v.tensor_reduce(badf[:, :], psum[0:1, 6 + p % 2, 256:256 + REP], AX.X, ALU.add))
                        link(v.tensor_copy(bad1[:, :], badf[:, :]))
                        dve.wait_ge(sm["expd"], REP * p + REP)
                        any_bad = dve.value_load(bad1[0:1, 0:1], min_val=0, max_val=P * REP)
                        c, pos, keep, cgt, r = (fb[:, j:j + 1] for j in range(5))
                        cur, bit, cand, sign, mask, one = (fbi[:, j:j + 1] for j in range(6))
                        z0, z1 = keys[:, 0, 0:w], keys[:, 1, 0:w]
                        with dve.If(any_bad > 0):
                            with dve.Fori(0, REP) as h:
                                def then(ins):
                                    dve.drain()
                                s = sc[:, p % 2, h, 0:w]
                                dve.drain()
                                then(v.memset(cur, 0))
                                then(v.memset(bit, 1 << 30))
                                then(v.tensor_scalar(z0, s, 0.0, None, ALU.is_ge, ALU.add, accum_out=c))
                                then(v.tensor_scalar(pos, c, kt, None, ALU.is_ge))
                                then(v.tensor_scalar(one, c, kt, None, ALU.is_lt))
                                then(v.tensor_scalar(sign, one, 31, None, ALU.logical_shift_left))
                                with dve.Fori(0, 31) as _:
                                    then(v.tensor_tensor(cand, cur, bit, ALU.bitwise_or))
                                    then(v.tensor_tensor(cand, cand, sign, ALU.bitwise_or))
                                    then(v.tensor_scalar(z0, s, cand.bitcast(F32), None, ALU.is_ge, ALU.add, accum_out=c))
                                    then(v.tensor_scalar(keep, c, kt, None, ALU.is_ge))
                                    then(v.tensor_tensor(mask, keep, pos, ALU.is_equal))
                                    then(v.tensor_scalar(mask, mask, 31, 31, ALU.logical_shift_left,
                                                         ALU.arith_shift_right))
                                    then(v.tensor_tensor(mask, mask, bit, ALU.bitwise_and))
                                    then(v.tensor_tensor(cur, cur, mask, ALU.bitwise_or))
                                    then(v.tensor_scalar(bit, bit, 1, None, ALU.logical_shift_right))
                                then(v.tensor_tensor(cand, cur, one, ALU.add))
                                then(v.tensor_tensor(cand, cand, sign, ALU.bitwise_or))
                                t = cand.bitcast(F32)
                                then(v.tensor_scalar(z0, s, t, None, ALU.is_gt, ALU.add, accum_out=cgt))
                                then(v.tensor_scalar(r, cgt, -1.0, kt, ALU.mult, ALU.add))
                                then(v.tensor_scalar(z0, s, t, None, ALU.is_equal))
                                then(v.tensor_tensor_scan(z1, z0, z0, 0.0, ALU.add, ALU.max))
                                then(v.scalar_tensor_tensor(z1, z1, r, z0, ALU.is_gt, ALU.mult))
                                then(v.scalar_tensor_tensor(s, z1, MASKED, s, ALU.mult, ALU.add))
                                then(v.tensor_copy(tt[:, p % 2, 3, bass.ds(h, 1)], t))

                    def probabilities(p):
                        w = widths(p)
                        top = ORDER[p] == 0
                        for h in range(REP):
                            dve.wait_ge(sm["expd"], REP * p + h + 1)
                            thr = b.tab[:, 0, TAB_OPEN:TAB_OPEN + 1] if top else tt[:, p % 2, 3, h:h + 1]
                            v.scalar_tensor_tensor(ex[:, h, 0:w], sc[:, p % 2, h, 0:w], thr, ex[:, h, 0:w],
                                                   ALU.is_ge, ALU.mult).then_inc(sm["prob"], 1)

                    def normalise(p):
                        dve.wait_ge(sm["pv"], blocks_before[p + 1])
                        acc = psum[:, 6 + p % 2, 0:REP * VW].rearrange("p (h d) -> p h d", h=REP)
                        link(v.reciprocal(rec[:, p % 2, :], acc[:, :, HD]))
                        if p >= 2:
                            dve.wait_ge(written[p % 2], 16 * (p // 2))
                        v.tensor_tensor(o_sb[:, p % 2, :, :], acc[:, :, 0:HD],
                                        rec[:, p % 2, :].rearrange("p (h o) -> p h o", o=1).broadcast_to([P, REP, HD]),
                                        ALU.mult).then_inc(sm["norm"], 1)

                    for p in range(TILES + 1):
                        if p >= 2:
                            normalise(p - 2)
                        for h in range(REP):
                            if p < TILES:
                                evacuate(p, h)
                            if p and ORDER[p - 1]:
                                if h == 0:
                                    dve.wait_ge(sm["t3"], p)
                                count(p - 1, h)
                        if p:
                            if ORDER[p - 1]:
                                select(p - 1)
                                fall_back(p - 1)
                                v.memset(fb[:, 15:16], 0.0).then_inc(sm["thr"], 1)
                            probabilities(p - 1)
                    normalise(TILES - 1)
            clear(nc, [*sm.values(), *written])


def build(nc, x, out, dram):
    with ExitStack() as ctx:
        sb = lambda n, s, d=F32: ctx.enter_context(nc.sbuf_tensor(n, s, d))
        for name, shape in (("x1", (S, D)), ("qkT", (QK, S)), ("attn", (S, D))):
            dram[name] = nc.dram_tensor(f"scratch_{name}", shape, F32, kind="Internal").ap()
        b = Names()
        b.psum = ctx.enter_context(nc.psum_tensor("banks", [P, 8, BANK], F32))
        b.eye = sb("eye", [P, P])
        b.future = sb("future", [P, P])
        b.steps = sb("steps", [P, 2 * REP * 8])
        b.tab = sb("tab", [P, TILES, TABS])
        b.ones = sb("ones", [P, P])
        b.mhalf = sb("mhalf", [P, 1])
        b.minus = sb("minus", [P, REP])
        b.router = sb("router", [P, DC, E])
        b.rbias = sb("rbias", [1, E])
        b.ebias = sb("ebias", [E, D])
        b.v_all = sb("v_all", [P, TILES, HKV, VW])
        b.t_all = sb("t_all", [P, TILES, H])
        b.slope_all = sb("slope_all", [P, TILES, H])
        phase_a(nc, b, x, dram)
        phase_b(nc, b, dram)
        phase_c(nc, b, dram, out)


def kernel(**inputs):
    import concourse.bacc as bacc
    from concourse.bass_utils import run_bass_kernel_spmd as run

    x = np.ascontiguousarray(inputs["L0_attn_hidden_states"]).reshape(S, D)
    arrays = {
        "x": x,
        "wqkv": np.ascontiguousarray(np.concatenate(
            [np.asarray(inputs[n]) for n in ("L0_attn_Wq", "L0_attn_Wk", "L0_attn_Wv")], 0).T),
        "wo": np.ascontiguousarray(np.asarray(inputs["L0_attn_Wo"]).T),
        "router": np.ascontiguousarray(np.asarray(inputs["L0_ffn_router_weight"]).T),
        "rbias": np.ascontiguousarray(inputs["L0_ffn_router_bias"]).reshape(1, E),
        "ebias": np.ascontiguousarray(inputs["L0_ffn_expert_bias"]),
        **shape_constants(),
    }
    nc = bacc.Bacc("TRN2", target_bir_lowering=False, num_devices=1)
    dram = {n: nc.dram_tensor(f"in_{n}", a.shape, F32, kind="ExternalInput").ap() for n, a in arrays.items()}
    out = nc.dram_tensor("out", (S, D), F32, kind="ExternalOutput").ap()
    build(nc, dram["x"], out, dram)
    r = run(nc, [{f"in_{n}": a for n, a in arrays.items()}], core_ids=[0])
    return np.asarray(r.results[0]["out"]).reshape(1, S, D)
```

```python
from contextlib import ExitStack
import math

import numpy as np

import concourse.bass as bass
from concourse import mybir

ALU = mybir.AluOpType
ACT = mybir.ActivationFunctionType
AX = mybir.AxisListType
F32 = mybir.dt.float32
BF16 = mybir.dt.bfloat16
I32 = mybir.dt.int32

P = 128
S, D = 2048, 1024
H, HKV, HD = 32, 8, 32
REP = H // HKV
E, TOP = 64, 8
KEEP = max(min(S, 128), S - int(S * 0.9))
THETA = 10000.0
EPS = 1e-5
SCALE = float(np.float32(1.0) / np.sqrt(np.float32(HD)))
TILES = S // P
DC = D // P
QK = (H + HKV) * HD
QKC = QK // P
QKV = QK + HKV * HD
PARTS = 3
VW = HD + 1
BANK = 512
MASKED = -2.0 ** 124
OPEN = -2.0 ** 123
WINDOW = 7
(TAB_Z, TAB_SLOPE, TAB_K, TAB_COUNT, TAB_OPEN, TAB_INVN, TABS) = range(7)
ORDER = list(range(1, TILES, 2)) + list(range(TILES - 2, -1, -2))
U = 2


def normal_point(p):
    lo, hi = -8.0, 8.0
    for _ in range(60):
        z = (lo + hi) / 2
        lo, hi = (z, hi) if 0.5 * (1 + math.erf(z / math.sqrt(2))) < p else (lo, z)
    return z


def shape_constants():
    inv = (np.float32(1.0) / np.float32(THETA) ** (np.arange(0, HD, 2, dtype=np.float32) / np.float32(HD)))
    angle = np.outer(np.arange(S, dtype=np.float32), inv.astype(np.float32)).astype(np.float32)
    angle = np.concatenate([angle, angle], -1)
    cos, sin = np.cos(angle), np.sin(angle)
    sin[:, :HD // 2] *= -1
    rope = np.concatenate([cos, sin], -1).astype(np.float32)
    tab = np.zeros((S, TABS), np.float32)
    for r in range(S):
        n, width = r + 1, P * (r // P + 1)
        k = min(KEEP, n)
        tab[r, TAB_K] = k
        tab[r, TAB_COUNT] = width / 2 - k
        tab[r, TAB_INVN] = 1.0 / width
        if n > KEEP:
            z = normal_point(1 - min(KEEP / (n + 0.5), 0.998))
            tab[r, TAB_Z] = z
            tab[r, TAB_SLOPE] = math.sqrt(2 * math.pi) * math.exp(z * z / 2) / n
        else:
            tab[r, TAB_OPEN] = OPEN
    eye = np.eye(P, dtype=np.float32)
    future = np.triu(np.full((P, P), MASKED, np.float32), 1)
    steps = np.tile(np.concatenate([np.tile(np.arange(8), REP), np.tile(np.arange(1, 9), REP)]), (P, 1)).astype(np.float32)
    return {"rope": rope, "tab": tab, "eye": eye, "future": future, "steps": steps}


def ffn_vector(nc, dve, link, t, sm, b):
    for j in range(2):
        nc.vector.bn_stats(b.stats[:, t, j * 6:j * 6 + 6], b.x[:, t, j * BANK:(j + 1) * BANK]).then_inc(sm["bn"], 1)
    yield
    dve.wait_ge(sm["bn"], 2 * t + 2)
    nc.vector.bn_aggr(b.mv[:, t, :], b.stats[:, t, :]).then_inc(sm["var"], 1)
    yield
    dve.wait_ge(sm["rstd"], t + 1)
    nc.vector.tensor_scalar(b.xn[:, t, :], b.x[:, t, :], b.mv[:, t, 0:1], b.rstd[:, t, 0:1],
                            ALU.subtract, ALU.mult).then_inc(sm["xn"], 1)
    yield
    dve.wait_ge(sm["logits"], t + 1)
    link(nc.vector.max(b.top[:, t, :], b.psum[:, 4 * t + 2, 0:E]))
    nc.vector.tensor_scalar(b.small[:, t, 0:1], b.top[:, t, 0:1], -1.0, None, ALU.mult).then_inc(sm["negmax"], 1)
    yield
    dve.wait_ge(sm["expd"], t + 1)
    link(nc.vector.max(b.top[:, t, :], b.e64[:, t, :]))
    nc.vector.match_replace(b.rest[:, t, :], b.top[:, t, :], b.e64[:, t, :], 0.0)
    nc.vector.tensor_reduce(b.small[:, t, 2:3], b.top[:, t, :], AX.X, ALU.add)
    link(nc.vector.reciprocal(b.small[:, t, 3:4], b.small[:, t, 1:2]))
    link(nc.vector.tensor_scalar(b.small[:, t, 4:5], b.small[:, t, 3:4], 0.5, None, ALU.mult))
    link(nc.vector.tensor_tensor(b.rest[:, t, :], b.e64[:, t, :], b.rest[:, t, :], ALU.subtract))
    nc.vector.tensor_scalar(b.mix[:, t, :], b.rest[:, t, :], b.small[:, t, 4:5], None, ALU.mult).then_inc(sm["mix"], 1)
    link(nc.vector.tensor_tensor(b.small[:, t, 5:6], b.small[:, t, 2:3], b.small[:, t, 4:5], ALU.mult))
    link(nc.vector.scalar_tensor_tensor(b.x[:, t, :], b.xn[:, t, :], b.small[:, t, 5:6], b.x[:, t, :], ALU.mult, ALU.add))
    yield
    dve.wait_ge(sm["mixed"], t + 1)
    nc.vector.tensor_tensor(b.x[:, t, :], b.x[:, t, :], bank2(b.psum, 4 * t), ALU.add).then_inc(sm["x1"], 1)
    yield


def bank2(psum, first, width=2 * BANK):
    return psum[:, first:first + 4, :].rearrange("p b n -> p (b n)")[:, 0:width]


def ffn_tensor(nc, pe, t, sm, b):
    transpose8(nc, pe, t, sm["xn"], t + 1, b, 4 * t, sm["xT"])
    yield
    pe.wait_ge(sm["xTcopy"], 2 * t + 2)
    logits = b.psum[:, 4 * t + 2, 0:E]
    for c in range(DC):
        nc.tensor.matmul(logits, b.xT[:, t, c, :], b.router[:, c, :], start=(c == 0), stop=False)
    nc.tensor.matmul(logits, b.ones[0:1, :], b.rbias[0:1, :], start=False, stop=True).then_inc(sm["logits"], 1)
    yield
    pe.wait_ge(sm["mix"], t + 1)
    nc.tensor.transpose(b.psum[0:E, 4 * t + 3, 0:P], b.mix[:, t, :], b.eye[:, :]).then_inc(sm["mixT"], 1)
    yield
    pe.wait_ge(sm["mixTcopy"], t + 1)
    for j in range(2):
        last = nc.tensor.matmul(b.psum[:, 4 * t + j, :], b.mixT[:, t, :], b.ebias[:, j * BANK:(j + 1) * BANK],
                                start=True, stop=True)
    last.then_inc(sm["mixed"], 1)
    yield


def transpose8(nc, pe, t, ready, count, b, bank, done):
    pe.wait_ge(ready, count)
    for c in range(DC):
        last = nc.tensor.transpose(b.psum[:, bank + c // 4, (c % 4) * P:(c % 4 + 1) * P],
                                   b.xn[:, t, c * P:(c + 1) * P], b.eye[:, :])
    last.then_inc(done, 1)


def ffn_scalar(nc, act, t, sm, b):
    act.wait_ge(sm["xT"], t + 1)
    copy_xT(nc, t, b, 4 * t, sm["xTcopy"])
    yield
    act.wait_ge(sm["negmax"], t + 1)
    nc.scalar.activation(b.e64[:, t, :], b.psum[:, 4 * t + 2, 0:E], ACT.Exp, bias=b.small[:, t, 0:1],
                         accum_out=b.small[:, t, 1:2]).then_inc(sm["expd"], 1)
    yield
    act.wait_ge(sm["mixT"], t + 1)
    nc.scalar.activation(b.mixT[:, t, :], b.psum[0:E, 4 * t + 3, 0:P], ACT.Copy).then_inc(sm["mixTcopy"], 1)
    yield


def copy_xT(nc, t, b, bank, done):
    for j in range(2):
        nc.scalar.activation(b.xT[:, t, 4 * j:4 * j + 4, :].rearrange("p c n -> p (c n)"),
                             b.psum[:, bank + j, :], ACT.Copy).then_inc(done, 1)


def rstd_pool(nc, pool, t, var, count, done, b):
    plink = b.plink
    pool.wait_ge(var, count)
    v, r, a = b.pw[:, t, 0:1], b.pw[:, t, 1:2], b.pw[:, t, 2:3]
    plink(nc.gpsimd.tensor_scalar(v, b.mv[:, t, 1:2], EPS, None, ALU.add))
    plink(nc.gpsimd.tensor_tensor(r, v, b.mhalf[:, 0:1], ALU.pow))
    plink(nc.gpsimd.tensor_tensor(a, r, r, ALU.mult))
    plink(nc.gpsimd.tensor_tensor(a, a, v, ALU.mult))
    plink(nc.gpsimd.tensor_scalar(a, a, -0.5, 1.5, ALU.mult, ALU.add))
    nc.gpsimd.tensor_tensor(b.rstd[:, t, 0:1], r, a, ALU.mult).then_inc(done, 1)


def interleave(parts):
    parts = list(parts)
    while parts:
        parts = [p for p in parts if next(p, "end") != "end"]


def flat(x):
    return x.rearrange("p c n -> p (c n)")


class Names:
    pass


def semaphores(nc, ctx, names, prefix):
    return {n: ctx.enter_context(nc.semaphore(f"{prefix}_{n}")) for n in names.split()}


def clear(nc, sems):
    nc.all_engine_barrier()
    for s in sems:
        nc.gpsimd.sem_clear(s)
    nc.all_engine_barrier()


def linker(engine, sem):
    count = [0]

    def link(ins):
        count[0] += 1
        ins.then_inc(sem, 1)
        engine.wait_ge(sem, count[0])
    return link


def ffn_buffers(nc, ctx, b, phase):
    sb = lambda n, s, d=F32: ctx.enter_context(nc.sbuf_tensor(f"{phase}_{n}", s, d))
    b.x = sb("x", [P, U, D])
    b.xn = sb("xn", [P, U, D])
    b.xT = sb("xT", [P, U, DC, P])
    b.stats = sb("stats", [P, U, 12])
    b.mv = sb("mv", [P, U, 2])
    b.rstd = sb("rstd", [P, U, 1])
    b.pw = sb("pw", [P, U, 4])
    b.small = sb("small", [P, U, 8])
    b.top = sb("top", [P, U, TOP])
    b.e64 = sb("e64", [P, U, E])
    b.rest = sb("rest", [P, U, E])
    b.mix = sb("mix", [P, U, E])
    b.mixT = sb("mixT", [E, U, P])


FFN_SEMS = "x bn var rstd xn xT xTcopy logits negmax expd mix mixT mixTcopy mixed x1 vchain pchain out "


def phase_a(nc, b, x_dram, dram):
    with ExitStack() as ctx:
        sb = lambda n, s, d=F32: ctx.enter_context(nc.sbuf_tensor(n, s, d))
        ffn_buffers(nc, ctx, b, "a")
        wqkv = sb("wqkv", [P, DC, QKV])
        rope = sb("rope", [P, U, 2 * HD])
        tab = sb("tab_a", [P, U, TABS])
        rot = sb("rot", [P, U, H + HKV, HD])
        qk = sb("qk", [P, U, H + HKV, HD])
        qkT = sb("qkT", [P, U, QKC, P])
        krep = sb("krep", [P, U, HKV, REP, HD], BF16)
        k1 = sb("k1", [P, U, HKV, VW], BF16)
        moments16 = sb("moments16", [P, U, HKV, VW], BF16)
        moments = sb("moments", [P, U, HKV, VW])
        prod = sb("prod", [P, U, H, HD])
        sums = sb("sums", [P, U, 2, H])
        gs = sb("gs", [P, U, 4, H])
        parts = sb("parts", [P, U, PARTS, QKC, P], BF16)
        left = sb("left", [P, U, QKC, P])

        su = semaphores(nc, ctx, "w fill", "sa")
        with nc.Block() as block:
            @block.sync
            def _(sp):
                sp.dma_start(wqkv[:, :, :], dram["wqkv"].rearrange("(c p) n -> p c n", p=P)).then_inc(su["w"], 16)
                sp.dma_start(b.router[:, :, :], dram["router"].rearrange("(c p) e -> p c e", p=P)).then_inc(su["w"], 16)
                sp.dma_start(b.ebias[:, :], dram["ebias"]).then_inc(su["w"], 16)
                sp.dma_start(b.rbias[:, :], dram["rbias"]).then_inc(su["w"], 16)
                sp.dma_start(b.eye[:, :], dram["eye"]).then_inc(su["w"], 16)
                sp.dma_start(b.future[:, :], dram["future"]).then_inc(su["w"], 16)
                sp.dma_start(b.steps[:, :], dram["steps"]).then_inc(su["w"], 16)
                sp.dma_start(b.tab[:, :, :], dram["tab"].rearrange("(t p) c -> p t c", p=P)).then_inc(su["w"], 16)
                sp.wait_ge(su["w"], 8 * 16)

            @block.vector
            def _(dve):
                nc.vector.memset(b.ones[:, :], 1.0)
                nc.vector.memset(b.mhalf[:, :], -0.5)
                nc.vector.memset(b.minus[:, :], -1.0)
                nc.vector.memset(moments[:, :, :, :], 0.0)
                nc.vector.memset(b.v_all[:, :, :, :], 1.0)
                nc.vector.memset(k1[:, :, :, :], 1.0).then_inc(su["fill"], 1)
                dve.wait_ge(su["w"], 8 * 16)
                nc.vector.tensor_copy(b.eye16[:, :], b.eye[:, :])
                nc.vector.tensor_copy(b.future16[:, :], b.future[:, :])

        with nc.Fori(0, TILES // U) as it, ExitStack() as ctx2:
            sm = semaphores(nc, ctx2, FFN_SEMS + "tabs x1out var2 rstd2 h hT hTcopy qkv cosd sind vcopy rot qkT "
                            "qkTcopy kk mom momsum y prod sums guess high left middle low deviation momcopy", "a")
            loaded = [ctx2.enter_context(nc.semaphore(f"a_load{t}")) for t in range(U)]
            with nc.Block() as block:
                @block.sync
                def _(sp):
                    for t in range(U):
                        rows = bass.ds((it * U + t) * P, P)
                        sp.dma_start(b.x[:, t, :], x_dram[rows, :]).then_inc(loaded[t], 16)
                        sp.dma_start(rope[:, t, :], dram["rope"][rows, :]).then_inc(loaded[t], 16)
                        sp.dma_start(tab[:, t, :], dram["tab"][rows, :]).then_inc(loaded[t], 16)
                    for t in range(U):
                        rows = bass.ds((it * U + t) * P, P)
                        sp.wait_ge(sm["x1"], t + 1)
                        sp.dma_start(dram["x1"][rows, :], b.x[:, t, :]).then_inc(sm["x1out"], 16)
                    for t in range(U):
                        for part, done in enumerate(("high", "middle", "low")):
                            sp.wait_ge(sm[done], (3 * t + 3) if part == 0 else t + 1)
                            for r in range(REP):
                                sp.dma_start(dram["qk_parts"][part, it * U + t, :, r::REP, :],
                                             parts[r * HD:(r + 1) * HD, t, part, :, :]).then_inc(sm["out"], 16)
                    sp.wait_ge(sm["x1out"], 16 * U)
                    sp.wait_ge(sm["out"], 16 * U * PARTS * REP)

                @block.tensor
                def _(pe):
                    def tile(t):
                        yield from ffn_tensor(nc, pe, t, sm, b)
                        transpose8(nc, pe, t, sm["h"], t + 1, b, 4 * t + 2, sm["hT"])
                        yield
                        pe.wait_ge(sm["hTcopy"], 2 * t + 2)
                        pe.wait_ge(sm["x1"], t + 1)
                        for c in range(DC):
                            for j in range(QKV // BANK):
                                last = nc.tensor.matmul(b.psum[:, 4 * t + j, :], b.xT[:, t, c, :],
                                                        wqkv[:, c, j * BANK:(j + 1) * BANK],
                                                        start=(c == 0), stop=(c == DC - 1))
                        last.then_inc(sm["qkv"], 1)
                        yield
                        pe.wait_ge(sm["rot"], t + 1)
                        pe.wait_ge(sm["vcopy"], t + 1)
                        for c in range(QKC):
                            last = nc.tensor.transpose(
                                b.psum[:, 4 * t + c // 4, (c % 4) * P:(c % 4 + 1) * P],
                                qk[:, t, 4 * c:4 * c + 4, :].rearrange("p h d -> p (h d)"), b.eye[:, :])
                        last.then_inc(sm["qkT"], 1)
                        yield
                        pe.wait_ge(sm["kk"], t + 1)
                        for g in range(HKV):
                            last = nc.tensor.matmul(b.psum[:, 4 * t + 3, g * VW:(g + 1) * VW],
                                                    krep[:, t, g, :, :].rearrange("p r d -> p (r d)"),
                                                    k1[:, t, g, :], start=True, stop=True)
                        last.then_inc(sm["mom"], 1)
                        yield
                        pe.wait_ge(sm["momcopy"], t + 1)
                        pe.wait_ge(sm["high"], 3 * t + 3)
                        for g in range(HKV):
                            for r in range(REP):
                                q = slice(r * HD, (r + 1) * HD)
                                last = nc.tensor.matmul(b.psum[:, 4 * t + r, g * VW:(g + 1) * VW], parts[q, t, 0, g, :],
                                                        moments16[q, t, g, :], start=True, stop=True)
                        last.then_inc(sm["y"], 1)
                        yield
                    interleave(tile(t) for t in range(U))

                @block.scalar
                def _(act):
                    def tile(t):
                        yield from ffn_scalar(nc, act, t, sm, b)
                        act.wait_ge(sm["hT"], t + 1)
                        act.wait_ge(sm["logits"], t + 1)
                        copy_xT(nc, t, b, 4 * t + 2, sm["hTcopy"])
                        yield
                        act.wait_ge(sm["qkv"], t + 1)
                        act.wait_ge(sm["sind"], 3 * t + 3)
                        nc.scalar.activation(b.v_all[:, it * U + t, :, 0:HD],
                                             b.psum[:, 4 * t + 2, 256:512].rearrange("p (g d) -> p g d", g=HKV),
                                             ACT.Copy).then_inc(sm["vcopy"], 1)
                        yield
                        act.wait_ge(sm["qkT"], t + 1)
                        for j, c in enumerate((0, 4, 8)):
                            w = min(4, QKC - c)
                            nc.scalar.activation(qkT[:, t, c:c + w, :].rearrange("p c n -> p (c n)"),
                                                 b.psum[:, 4 * t + j, 0:w * P], ACT.Copy).then_inc(sm["qkTcopy"], 1)
                            nc.scalar.activation(parts[:, t, 0, c:c + w, :].rearrange("p c n -> p (c n)"),
                                                 b.psum[:, 4 * t + j, 0:w * P], ACT.Copy).then_inc(sm["high"], 1)
                        yield
                        act.wait_ge(sm["left"], t + 1)
                        nc.scalar.activation(flat(parts[:, t, 1, :, :]), flat(left[:, t, :, :]), ACT.Copy)\
                            .then_inc(sm["middle"], 1)
                        yield
                    interleave(tile(t) for t in range(U))

                @block.gpsimd
                def _(pool):
                    b.plink = plink = linker(pool, sm["pchain"])

                    def tile(t):
                        rstd_pool(nc, pool, t, sm["var"], t + 1, sm["rstd"], b)
                        yield
                        pool.wait_ge(sm["xn"], t + 1)
                        rstd_pool(nc, pool, t, sm["var2"], t + 1, sm["rstd2"], b)
                        yield
                        pool.wait_ge(sm["rot"], t + 1)
                        for r in range(REP):
                            nc.gpsimd.tensor_copy(krep[:, t, :, r, :], qk[:, t, H:, :])
                        nc.gpsimd.tensor_copy(k1[:, t, :, 0:HD], qk[:, t, H:, :]).then_inc(sm["kk"], 1)
                        yield
                        pool.wait_ge(sm["deviation"], t + 1)
                        mean, sq, t0, sl = (gs[:, t, j, :] for j in range(4))
                        col = lambda c: tab[:, t, c:c + 1]
                        plink(nc.gpsimd.tensor_scalar(t0, sq, col(TAB_Z), None, ALU.mult))
                        plink(nc.gpsimd.tensor_tensor(t0, t0, mean, ALU.add))
                        plink(nc.gpsimd.tensor_scalar(t0, t0, col(TAB_OPEN), None, ALU.add))
                        plink(nc.gpsimd.tensor_scalar(sl, sq, col(TAB_SLOPE), None, ALU.mult))
                        nc.gpsimd.tensor_copy(b.t_all[:, it * U + t, :], t0)
                        nc.gpsimd.tensor_copy(b.slope_all[:, it * U + t, :], sl).then_inc(sm["guess"], 1)
                        yield
                    interleave(tile(t) for t in range(U))

                @block.vector
                def _(dve):
                    link = linker(dve, sm["vchain"])

                    def tile(t):
                        dve.wait_ge(loaded[t], 48)
                        yield from ffn_vector(nc, dve, link, t, sm, b)
                        dve.wait_ge(sm["x1"], t + 1)
                        for j in range(2):
                            last = nc.vector.bn_stats(b.stats[:, t, j * 6:j * 6 + 6],
                                                      b.x[:, t, j * BANK:(j + 1) * BANK])
                            if j:
                                link(last)
                        nc.vector.bn_aggr(b.mv[:, t, :], b.stats[:, t, :]).then_inc(sm["var2"], 1)
                        yield
                        dve.wait_ge(sm["rstd2"], t + 1)
                        dve.wait_ge(sm["xT"], t + 1)
                        nc.vector.tensor_scalar(b.xn[:, t, :], b.x[:, t, :], b.mv[:, t, 0:1], b.rstd[:, t, 0:1],
                                                ALU.subtract, ALU.mult).then_inc(sm["h"], 1)
                        yield
                        dve.wait_ge(sm["qkv"], t + 1)
                        proj = bank2(b.psum, 4 * t, QK).rearrange("p (h d) -> p h d", d=HD)
                        lo, hi = slice(0, HD // 2), slice(HD // 2, HD)
                        cos = rope[:, t:t + 1, 0:HD].broadcast_to([P, H + HKV, HD])
                        sin = rope[:, t:t + 1, HD:2 * HD]
                        nc.vector.tensor_tensor(qk[:, t, :, :], proj, cos, ALU.mult).then_inc(sm["sind"], 1)
                        nc.vector.tensor_tensor(rot[:, t, :, lo], proj[:, :, hi],
                                                sin[:, :, lo].broadcast_to([P, H + HKV, HD // 2]),
                                                ALU.mult).then_inc(sm["sind"], 1)
                        nc.vector.tensor_tensor(rot[:, t, :, hi], proj[:, :, lo],
                                                sin[:, :, hi].broadcast_to([P, H + HKV, HD // 2]),
                                                ALU.mult).then_inc(sm["sind"], 1)
                        dve.wait_ge(sm["sind"], 3 * t + 3)
                        nc.vector.tensor_tensor(qk[:, t, :, :], qk[:, t, :, :], rot[:, t, :, :],
                                                ALU.add).then_inc(sm["rot"], 1)
                        yield
                        dve.wait_ge(sm["high"], 3 * t + 3)
                        nc.vector.tensor_tensor(flat(left[:, t, :, :]), flat(qkT[:, t, :, :]),
                                                flat(parts[:, t, 0, :, :]), ALU.subtract).then_inc(sm["left"], 1)
                        yield
                        dve.wait_ge(sm["middle"], t + 1)
                        nc.vector.tensor_tensor(flat(parts[:, t, 2, :, :]), flat(left[:, t, :, :]),
                                                flat(parts[:, t, 1, :, :]), ALU.subtract).then_inc(sm["low"], 1)
                        dve.wait_ge(sm["mom"], t + 1)
                        if t:
                            dve.wait_ge(sm["momsum"], t)
                        nc.vector.tensor_tensor(moments[:, t, :, :], moments[:, 1 - t, :, :],
                                                b.psum[:, 4 * t + 3, 0:HKV * VW].rearrange("p (g d) -> p g d", g=HKV),
                                                ALU.add).then_inc(sm["momsum"], 1)
                        dve.wait_ge(sm["momsum"], t + 1)
                        nc.vector.tensor_copy(moments16[:, t, :, :], moments[:, t, :, :]).then_inc(sm["momcopy"], 1)
                        yield
                        dve.wait_ge(sm["y"], t + 1)
                        for r in range(REP):
                            y = b.psum[:, 4 * t + r, 0:HKV * VW].rearrange("p (g d) -> p g d", g=HKV)
                            copied = nc.vector.tensor_copy(sums[:, t, 1, r::REP], y[:, :, HD])
                            last = nc.vector.tensor_tensor(prod[:, t, r::REP, :], y[:, :, 0:HD], qk[:, t, r:H:REP, :],
                                                           ALU.mult)
                        copied.then_inc(sm["sums"], 1)
                        link(last)
                        link(nc.vector.tensor_reduce(sums[:, t, 0, :], prod[:, t, :, :], AX.X, ALU.add))
                        dve.wait_ge(sm["sums"], t + 1)
                        e2, s1 = sums[:, t, 0, :], sums[:, t, 1, :]
                        mean, sq, var, half = (gs[:, t, j, :] for j in range(4))
                        n = tab[:, t, TAB_INVN:TAB_INVN + 1]
                        link(nc.vector.tensor_scalar(mean, s1, n, None, ALU.mult))
                        link(nc.vector.tensor_tensor(sq, mean, mean, ALU.mult))
                        link(nc.vector.scalar_tensor_tensor(var, e2, n, sq, ALU.mult, ALU.subtract))
                        link(nc.vector.tensor_scalar(var, var, 1e-30, None, ALU.max))
                        link(nc.vector.tensor_scalar(sq.bitcast(I32), var.bitcast(I32), 0.5, float(0x1FBD0000),
                                                     ALU.mult, ALU.add))
                        for last in (False, True):
                            link(nc.vector.reciprocal(half, sq))
                            link(nc.vector.tensor_tensor(half, half, var, ALU.mult))
                            link(nc.vector.tensor_tensor(half, half, sq, ALU.add))
                            step = nc.vector.tensor_scalar(sq, half, 0.5, None, ALU.mult)
                            if last:
                                step.then_inc(sm["deviation"], 1)
                            else:
                                link(step)
                        yield
                    interleave(tile(t) for t in range(U))
            clear(nc, [*sm.values(), *loaded])


def phase_c(nc, b, dram, out):
    with ExitStack() as ctx:
        sb = lambda n, s, d=F32: ctx.enter_context(nc.sbuf_tensor(n, s, d))
        ffn_buffers(nc, ctx, b, "c")
        wo = sb("wo", [P, DC, D])
        su = semaphores(nc, ctx, "w", "sc")
        with nc.Block() as block:
            @block.sync
            def _(sp):
                sp.dma_start(wo[:, :, :], dram["wo"].rearrange("(c p) n -> p c n", p=P)).then_inc(su["w"], 16)
                sp.wait_ge(su["w"], 16)

        with nc.Fori(0, TILES // U) as it, ExitStack() as ctx2:
            sm = semaphores(nc, ctx2, FFN_SEMS + "aT aTcopy proj xsum", "c")
            loaded = [ctx2.enter_context(nc.semaphore(f"c_load{t}")) for t in range(U)]
            with nc.Block() as block:
                @block.sync
                def _(sp):
                    for t in range(U):
                        rows = bass.ds((it * U + t) * P, P)
                        sp.dma_start(b.xn[:, t, :], dram["attn"][rows, :]).then_inc(loaded[t], 16)
                        sp.dma_start(b.x[:, t, :], dram["x1"][rows, :]).then_inc(loaded[t], 16)
                    for t in range(U):
                        rows = bass.ds((it * U + t) * P, P)
                        sp.wait_ge(sm["x1"], t + 1)
                        sp.dma_start(out[rows, :], b.x[:, t, :]).then_inc(sm["out"], 16)
                    sp.wait_ge(sm["out"], 16 * U)

                @block.tensor
                def _(pe):
                    def tile(t):
                        transpose8(nc, pe, t, loaded[t], 32, b, 4 * t + 2, sm["aT"])
                        yield
                        pe.wait_ge(sm["aTcopy"], 2 * t + 2)
                        for c in range(DC):
                            for j in range(2):
                                last = nc.tensor.matmul(b.psum[:, 4 * t + j, :], b.xT[:, t, c, :],
                                                        wo[:, c, j * BANK:(j + 1) * BANK],
                                                        start=(c == 0), stop=(c == DC - 1))
                        last.then_inc(sm["proj"], 1)
                        yield
                        yield from ffn_tensor(nc, pe, t, sm, b)
                    interleave(tile(t) for t in range(U))

                @block.scalar
                def _(act):
                    def tile(t):
                        act.wait_ge(sm["aT"], t + 1)
                        copy_xT(nc, t, b, 4 * t + 2, sm["aTcopy"])
                        yield
                        act.wait_ge(sm["proj"], t + 1)
                        yield from ffn_scalar(nc, act, t, sm, b)
                    interleave(tile(t) for t in range(U))

                @block.gpsimd
                def _(pool):
                    b.plink = linker(pool, sm["pchain"])

                    def tile(t):
                        rstd_pool(nc, pool, t, sm["var"], t + 1, sm["rstd"], b)
                        yield
                    interleave(tile(t) for t in range(U))

                @block.vector
                def _(dve):
                    link = linker(dve, sm["vchain"])

                    def tile(t):
                        dve.wait_ge(loaded[t], 32)
                        dve.wait_ge(sm["proj"], t + 1)
                        link(nc.vector.tensor_tensor(b.x[:, t, :], b.x[:, t, :], bank2(b.psum, 4 * t), ALU.add))
                        yield
                        yield from ffn_vector(nc, dve, link, t, sm, b)
                    interleave(tile(t) for t in range(U))
            clear(nc, [*sm.values(), *loaded])


def uses_of_slots():
    return [(p, h, c, min(2 * BANK, P * (i + 1) - 2 * BANK * c))
            for p, i in enumerate(ORDER) for h in range(REP) for c in range(-(-P * (i + 1) // (2 * BANK)))]


AMONG = 0.1

Q_ROWS = ((0, 0, 1, 1), (0, 2, 1, 2))
K_ROWS = ((0, 1, 0, 1), (2, 0, 2, 1))


def phase_b(nc, b, dram):
    uses = uses_of_slots()
    evacuated = {}
    for n, (p, h, c, w) in enumerate(uses):
        evacuated[p, h] = n + 1
    chunks = [-(-P * (i + 1) // (2 * BANK)) for i in ORDER]
    blocks_before = [sum(ORDER[q] + 1 for q in range(p)) for p in range(TILES + 1)]
    full = P * TILES

    with ExitStack() as ctx:
        sb = lambda n, s, d=F32: ctx.enter_context(nc.sbuf_tensor(n, s, d))
        q_sb = sb("q_sb", [P, 2, 2, REP, P], BF16)
        k_sb = sb("k_sb", [P, 2, TILES, P], BF16)
        v_sb = sb("v_sb", [P, TILES, VW])
        tg = sb("tg", [P, TILES, REP])
        slg = sb("slg", [P, TILES, REP])
        sc = sb("sc", [P, 3, REP, S])
        ex = sb("ex", [P, REP, S])
        keys = sb("keys", [P, S])
        junk = sb("junk", [P, 2, S], BF16)
        passed = sb("passed", [P, S], BF16)
        pT = sb("pT", [P, 3, REP * P])
        mx = sb("mx", [P, 3, 2, REP])
        nmx = sb("nmx", [P, 2, REP])
        sgn = sb("sgn", [P, 2, 3, REP])
        tt = sb("tt", [P, 2, 4, REP])
        dd = sb("dd", [P, 2, 3, REP])
        pw = sb("pw_b", [P, 8, REP])
        cnt = sb("cnt", [P, 2, REP])
        d = sb("d", [P, REP])
        js = sb("js", [P, 6, REP])
        sel = sb("sel", [P, 2, REP, 8])
        dirn = sb("dirn", [P, REP], I32)
        flip = sb("flip", [P, REP], I32)
        near = sb("near", [P, REP, 8])
        pick = sb("pick", [P, 2, REP, 8])
        dk = sb("dk", [P, 2, REP])
        gap = sb("gap", [P, 4, REP])
        bad = sb("bad", [P, REP])
        badh = sb("badh", [1, REP], I32)
        badf = sb("badf", [1, 1])
        bad1 = sb("bad1", [1, 1], I32)
        rec = sb("rec", [P, 2, REP])
        o_sb = sb("o_sb", [P, 2, REP, HD])
        fb = sb("fb", [P, 8])
        fbi = sb("fbi", [P, 8], I32)
        psum = b.psum

        def slot(n):
            return bank2(psum, 2 * (n % 2))

        def width(p):
            return P * (ORDER[p] + 1)

        def wide(x):
            return x.rearrange("p (h o) -> p h o", o=1).broadcast_to([P, REP, 8])

        def share(p, low, high):
            nb = ORDER[p] + 1
            return range(round(nb * low), round(nb * high))

        with nc.Fori(0, HKV) as g, ExitStack() as ctx2:
            sm = semaphores(nc, ctx2, "k vt s evac nmx t1 t2 t3 expd vchain pchain dist thr sel prob pT "
                            "pTcopy pv bad badsum norm junk", "b")
            loaded = [ctx2.enter_context(nc.semaphore(f"b_q{n}")) for n in range(2)]
            written = [ctx2.enter_context(nc.semaphore(f"b_written{n}")) for n in range(2)]
            with nc.Block() as block:
                def store(sp, p):
                    sp.wait_ge(sm["norm"], p + 1)
                    sp.dma_start(dram["attn"][ORDER[p] * P:(ORDER[p] + 1) * P, bass.ds(g * P, P)],
                                 o_sb[:, p % 2, :, :].rearrange("p h d -> p (h d)")).then_inc(written[p % 2], 16)

                @block.sync
                def _(sp):
                    parts = dram["qk_parts"]

                    def load_q(p):
                        if p >= 2:
                            sp.wait_ge(sm["s"], evacuated[p - 2, REP - 1])
                        for m in range(2):
                            for r in range(4):
                                sp.dma_start(q_sb[r * HD:(r + 1) * HD, p % 2, m, :, :],
                                             parts[Q_ROWS[m][r], ORDER[p], :, bass.ds(g * REP, REP), :])\
                                    .then_inc(loaded[p % 2], 16)

                    for m in range(2):
                        for r in range(4):
                            sp.dma_start(k_sb[r * HD:(r + 1) * HD, m, :, :],
                                         parts[K_ROWS[m][r], :, :, bass.ds(g + H, 1), :]
                                         .rearrange("t d o s -> d t (o s)")).then_inc(sm["k"], 16)
                    load_q(0)
                    load_q(1)
                    for p, i in enumerate(ORDER):
                        if p + 2 < TILES:
                            load_q(p + 2)
                        if p:
                            store(sp, p - 1)
                    store(sp, TILES - 1)
                    for w in written:
                        sp.wait_ge(w, 16 * TILES // 2)

                @block.tensor
                def _(pe):
                    pe.wait_ge(sm["k"], 16 * 8)
                    pe.wait_ge(sm["vt"], 3)

                    def scores(p, h):
                        if h == 0:
                            pe.wait_ge(loaded[p % 2], 16 * 8 * (p // 2 + 1))
                        for n, (pp, hh, c, w) in enumerate(uses):
                            if (pp, hh) != (p, h):
                                continue
                            if n >= 2:
                                pe.wait_ge(sm["evac"], n - 1)
                            for j in range(0, w, BANK):
                                wj = min(BANK, w - j)
                                col = c * 2 * BANK + j
                                diag = col + wj == width(p)
                                for m in range(2):
                                    last = nc.tensor.matmul(slot(n)[:, j:j + wj], q_sb[:, p % 2, m, h, :],
                                                            flat(k_sb[:, m, :, :])[:, col:col + wj],
                                                            start=(m == 0), stop=(m == 1 and not diag))
                                if diag:
                                    last = nc.tensor.matmul(slot(n)[:, j + wj - P:j + wj], b.eye16[:, :],
                                                            b.future16[:, :], start=False, stop=True)
                            last.then_inc(sm["s"], 1)

                    def flags(p):
                        pe.wait_ge(sm["bad"], p + 1)
                        nc.tensor.matmul(psum[0:1, 7, 256:256 + REP], b.ones[:, 0:1], bad[:, :],
                                         start=True, stop=True).then_inc(sm["badsum"], 1)

                    def turn(p, kb):
                        n = blocks_before[p] + kb
                        if n >= 2:
                            pe.wait_ge(sm["pTcopy"], n - 1)
                        for h in range(REP):
                            last = nc.tensor.transpose(psum[:, 4 + n % 2, h * P:(h + 1) * P],
                                                       sc[:, p % 3, h, kb * P:(kb + 1) * P], b.eye[:, :])
                        last.then_inc(sm["pT"], 1)

                    def product(p, kb):
                        n = blocks_before[p] + kb
                        pe.wait_ge(sm["pTcopy"], n + 1)
                        if kb == 0 and p:
                            pe.wait_ge(sm["norm"], p)
                        for h in range(REP):
                            last = nc.tensor.matmul(psum[:, 6, h * VW:(h + 1) * VW],
                                                    pT[:, n % 3, h * P:(h + 1) * P], v_sb[:, kb, :],
                                                    start=(kb == 0 and h == 0), stop=(kb == ORDER[p]),
                                                    skip_group_check=True)
                        last.then_inc(sm["pv"], 1)

                    def values(p, blocks):
                        for kb in blocks:
                            turn(p, kb)
                            if kb:
                                product(p, kb - 1)

                    for p in range(TILES + 2):
                        for h in range(REP):
                            if p < TILES:
                                scores(p, h)
                            if p >= 2:
                                if h == 0:
                                    pe.wait_ge(sm["prob"], REP * (p - 1))
                                values(p - 2, share(p - 2, AMONG * h / REP, AMONG * (h + 1) / REP))
                        if p >= 2:
                            values(p - 2, share(p - 2, AMONG, 1))
                            product(p - 2, ORDER[p - 2])
                        if 1 <= p <= TILES and ORDER[p - 1]:
                            flags(p - 1)

                @block.scalar
                def _(act):
                    signs = [0]

                    def count(p, h, k, t):
                        n = signs[0]
                        signs[0] += 1
                        if n >= 2:
                            act.wait_ge(sm["junk"], n - 1)
                        w = width(p)
                        nc.scalar.activation(junk[:, n % 2, 0:w], sc[:, p % 3, h, 0:w], ACT.Sign, bias=t, scale=-1.0,
                                             accum_out=sgn[:, p % 2, k, h:h + 1]).then_inc(sm["junk"], 1)

                    def exponentials(p, heads):
                        if heads[0] == 0:
                            act.wait_ge(sm["nmx"], p + 1)
                            if p:
                                act.wait_ge(sm["prob"], REP * p)
                        for h in heads:
                            w = width(p)
                            nc.scalar.activation(ex[:, h, 0:w], sc[:, p % 3, h, 0:w], ACT.Exp,
                                                 bias=nmx[:, p % 2, h:h + 1], scale=SCALE).then_inc(sm["expd"], 1)

                    def copies(p, low, high):
                        if p < 0:
                            return
                        for kb in share(p, low, high):
                            n = blocks_before[p] + kb
                            act.wait_ge(sm["pT"], n + 1)
                            if n >= 3:
                                act.wait_ge(sm["pv"], n - 2)
                            nc.scalar.activation(pT[:, n % 3, :], psum[:, 4 + n % 2, :], ACT.Copy)\
                                .then_inc(sm["pTcopy"], 1)

                    for p in range(TILES + 2):
                        new = p < TILES and ORDER[p]
                        for h in range(REP):
                            if new:
                                act.wait_ge(sm["evac"], evacuated[p, h])
                                if h == 0:
                                    act.wait_ge(sm["vt"], 3)
                                count(p, h, 0, tg[:, ORDER[p], h:h + 1])
                            copies(p - 2, AMONG * h / REP, AMONG * (h + 1) / REP)
                        n, copying = 0, 9
                        for k in (1, 2):
                            for h in (2 * k - 2, 2 * k - 1):
                                if 1 <= p <= TILES:
                                    exponentials(p - 1, (h,))
                                copies(p - 2, AMONG + (1 - AMONG) * min(n / copying, 1),
                                       AMONG + (1 - AMONG) * min((n + 1) / copying, 1))
                                n += 1
                            for h in range(REP):
                                if new:
                                    if h == 0:
                                        act.wait_ge(sm[f"t{k}"], p + 1)
                                    count(p, h, k, tt[:, p % 2, k - 1, h:h + 1])
                                copies(p - 2, AMONG + (1 - AMONG) * min(n / copying, 1),
                                       AMONG + (1 - AMONG) * min((n + 1) / copying, 1))
                                n += 1

                @block.gpsimd
                def _(pool):
                    link = linker(pool, sm["pchain"])
                    gp = nc.gpsimd
                    gp.tensor_copy(v_sb[:, :, :], b.v_all[:, :, g, :]).then_inc(sm["vt"], 1)
                    gp.tensor_copy(tg[:, :, :], b.t_all[:, :, bass.ds(g * REP, REP)]).then_inc(sm["vt"], 1)
                    gp.tensor_copy(slg[:, :, :], b.slope_all[:, :, bass.ds(g * REP, REP)]).then_inc(sm["vt"], 1)
                    pool.wait_ge(sm["vt"], 3)

                    def update(p, k, done):
                        i = ORDER[p]
                        before = tg[:, i, :] if k == 0 else tt[:, p % 2, k - 1, :]
                        dist = dd[:, p % 2, k, :]
                        st = slg[:, i, :]
                        gate, move, den, s, lo = (pw[:, j, :] for j in range(5))
                        link(gp.tensor_scalar(dist, sgn[:, p % 2, k, :], -0.5, b.tab[:, i, TAB_COUNT:TAB_COUNT + 1],
                                              ALU.mult, ALU.add))
                        link(gp.tensor_tensor(gate, dist, dist, ALU.mult))
                        link(gp.tensor_scalar(gate, gate, (WINDOW - 0.4) ** 2, None, ALU.is_gt))
                        if k == 0:
                            link(gp.tensor_tensor(move, dist, st, ALU.mult))
                        else:
                            older = tg[:, i, :] if k == 1 else tt[:, p % 2, k - 2, :]
                            link(gp.tensor_tensor(den, dd[:, p % 2, k - 1, :], dist, ALU.subtract))
                            link(gp.tensor_tensor(s, before, older, ALU.subtract))
                            link(gp.tensor_tensor(s, s, den, ALU.mult))
                            link(gp.tensor_tensor(den, den, den, ALU.mult))
                            link(gp.tensor_scalar(den, den, 0.25, None, ALU.max))
                            link(gp.tensor_scalar(lo, st, 1e-30, None, ALU.max))
                            link(gp.tensor_tensor(den, den, lo, ALU.mult))
                            link(gp.tensor_tensor(den, den, b.minus[:, :], ALU.pow))
                            link(gp.tensor_tensor(s, s, den, ALU.mult))
                            link(gp.tensor_scalar(s, s, 0.5, 2.0, ALU.max, ALU.min))
                            link(gp.tensor_tensor(s, s, st, ALU.mult))
                            link(gp.tensor_tensor(move, dist, s, ALU.mult))
                        link(gp.tensor_tensor(move, move, gate, ALU.mult))
                        gp.tensor_tensor(tt[:, p % 2, k, :], before, move, ALU.add).then_inc(done, 1)

                    def selectors(p):
                        pool.wait_ge(sm["dist"], p + 1)
                        if p:
                            pool.wait_ge(sm["sel"], 2 * p)
                        a, j1, j2, nz, x = (js[:, j, :] for j in range(5))
                        steps = [b.steps[:, m * REP * 8:(m + 1) * REP * 8].rearrange("p (h o) -> p h o", h=REP)
                                 for m in range(2)]
                        link(gp.tensor_scalar(x, d[:, :], 0.0, None, ALU.is_ge))
                        link(gp.tensor_scalar(x, x, 2.0, -1.0, ALU.mult, ALU.add))
                        link(gp.tensor_tensor(a, d[:, :], x, ALU.mult))
                        link(gp.tensor_scalar(x, x, 0.5, -0.5, ALU.mult, ALU.add))
                        link(gp.tensor_tensor(j1, a, x, ALU.add))
                        link(gp.tensor_scalar(j2, a, 2.0, None, ALU.mult))
                        link(gp.tensor_tensor(j2, j2, j1, ALU.subtract))
                        link(gp.tensor_scalar(nz, a, 0.0, None, ALU.is_gt))
                        for m, j in enumerate((j1, j2)):
                            e = sel[:, m, :, :]
                            link(gp.tensor_tensor(e, steps[m], wide(j), ALU.subtract))
                            link(gp.tensor_scalar(e, e, 0.0, None, ALU.is_equal))
                            gp.tensor_tensor(e, e, wide(nz), ALU.mult).then_inc(sm["sel"], 1)

                    rounds = 0
                    for p in range(TILES + 1):
                        if p < TILES:
                            pool.wait_ge(sm["evac"], evacuated[p, REP - 1])
                            if p >= 2:
                                pool.wait_ge(sm["expd"], REP * (p - 1))
                            gp.tensor_scalar(nmx[:, p % 2, :], mx[:, p % 3, chunks[p] - 1, :], -SCALE, None,
                                             ALU.mult).then_inc(sm["nmx"], 1)
                        new = p < TILES and ORDER[p]
                        if new:
                            if p >= 2:
                                pool.wait_ge(sm["thr"], p - 1)
                            rounds += REP
                            pool.wait_ge(sm["junk"], rounds)
                            update(p, 0, sm["t1"])
                        if p and ORDER[p - 1]:
                            selectors(p - 1)
                        if new:
                            for k, done in ((1, sm["t2"]), (2, sm["t3"])):
                                rounds += REP
                                pool.wait_ge(sm["junk"], rounds)
                                update(p, k, done)

                @block.vector
                def _(dve):
                    link = linker(dve, sm["vchain"])
                    v = nc.vector
                    dve.wait_ge(sm["vt"], 3)

                    def evacuate(p, h):
                        for n, (pp, hh, c, w) in enumerate(uses):
                            if (pp, hh) != (p, h):
                                continue
                            dve.wait_ge(sm["s"], n + 1)
                            if p >= 3 and h == 0 and c == 0:
                                dve.wait_ge(sm["nmx"], p - 2)
                                dve.wait_ge(sm["pT"], blocks_before[p - 2])
                            if c:
                                dve.wait_ge(sm["evac"], n)
                            v.tensor_scalar(sc[:, p % 3, h, c * 2 * BANK:c * 2 * BANK + w], slot(n)[:, 0:w], 0.0,
                                            mx[:, p % 3, 0, h:h + 1] if c else None, ALU.add, ALU.max,
                                            accum_out=mx[:, p % 3, c, h:h + 1]).then_inc(sm["evac"], 1)

                    def count(p, h):
                        if h == 0:
                            dve.wait_ge(sm["t3"], p + 1)
                        w = width(p)
                        link(v.tensor_scalar(passed[:, 0:w], sc[:, p % 3, h, 0:w], tt[:, p % 2, 2, h:h + 1],
                                             None, ALU.is_ge, ALU.add, accum_out=cnt[:, p % 2, h:h + 1]))

                    def select(p):
                        i, w = ORDER[p], width(p)
                        t3 = tt[:, p % 2, 2, :]
                        kt = b.tab[:, i, TAB_K:TAB_K + 1]
                        if p:
                            dve.wait_ge(sm["sel"], 2 * p)
                        v.tensor_scalar(d[:, :], cnt[:, p % 2, :], kt, None, ALU.subtract).then_inc(sm["dist"], 1)
                        dve.wait_ge(sm["dist"], p + 1)
                        link(v.tensor_scalar(dirn[:, :], d[:, :], 0.0, None, ALU.is_gt))
                        link(v.tensor_scalar(flip[:, :], dirn[:, :], 29, 0x1FFFFFFF, ALU.logical_shift_left,
                                             ALU.bitwise_or))
                        for h in range(REP):
                            z = keys[:, 0:w]
                            link(v.tensor_scalar(z, sc[:, p % 3, h, 0:w], t3[:, h:h + 1], None, ALU.subtract))
                            link(v.tensor_scalar(z.bitcast(I32), z.bitcast(I32), 2, flip[:, h:h + 1],
                                                 ALU.logical_shift_right, ALU.bitwise_xor))
                            link(v.max(near[:, h, :], z))
                        bits = near[:, :, :].bitcast(I32)
                        link(v.tensor_tensor(bits, bits, wide(flip[:, :]), ALU.bitwise_xor))
                        link(v.tensor_scalar(bits, bits, 2, None, ALU.logical_shift_left))
                        dve.wait_ge(sm["sel"], 2 * p + 2)
                        twice = near[:, :, :].rearrange("p (o h) e -> p o (h e)", o=1).broadcast_to([P, 2, REP * 8])
                        link(v.tensor_tensor(pick[:, :, :, :].rearrange("p o h e -> p o (h e)"),
                                             sel[:, :, :, :].rearrange("p o h e -> p o (h e)"), twice, ALU.mult))
                        link(v.tensor_reduce(dk[:, :, :], pick[:, :, :, :], AX.X, ALU.add))
                        kth, nxt = dk[:, 0, :], dk[:, 1, :]
                        g0, g1, g2, g3 = (gap[:, j, :] for j in range(4))
                        link(v.tensor_tensor(g0, kth, nxt, ALU.subtract))
                        link(v.tensor_scalar(g1, g0, 2.0 ** 100, -2.0 ** 19, ALU.min, ALU.mult))
                        link(v.tensor_tensor(g2, g1, kth, ALU.subtract))
                        link(v.tensor_tensor(g1, g1, kth, ALU.add))
                        link(v.tensor_tensor(g1, g1, g2, ALU.max))
                        link(v.tensor_scalar(g1, g1, 0.0, None, ALU.is_ge))
                        link(v.tensor_tensor(g2, d[:, :], d[:, :], ALU.mult))
                        link(v.scalar_tensor_tensor(g1, g2, 0.5, g1, ALU.is_gt, ALU.mult))
                        if p:
                            dve.wait_ge(sm["badsum"], p)
                        v.scalar_tensor_tensor(bad[:, :], g2, (WINDOW + 0.5) ** 2, g1, ALU.is_gt, ALU.max)\
                            .then_inc(sm["bad"], 1)
                        link(v.scalar_tensor_tensor(g3, g0, -0.25, kth, ALU.mult, ALU.add))
                        link(v.tensor_tensor(tt[:, p % 2, 3, :], t3, g3, ALU.add))

                    def fall_back(p):
                        i, w = ORDER[p], width(p)
                        kt = b.tab[:, i, TAB_K:TAB_K + 1]
                        dve.wait_ge(sm["badsum"], p + 1)
                        v.tensor_copy(badh[:, :], psum[0:1, 7, 256:256 + REP])
                        link(v.tensor_reduce(badf[:, :], psum[0:1, 7, 256:256 + REP], AX.X, ALU.add))
                        link(v.tensor_copy(bad1[:, :], badf[:, :]))
                        dve.wait_ge(sm["expd"], REP * p + REP)
                        c, pos, cgt, r = (fb[:, j:j + 1] for j in range(4))
                        cur, bit, cand, sign, mask, one = (fbi[:, j:j + 1] for j in range(6))
                        z0, z1 = passed[:, 0:w], keys[:, 0:w]
                        any_bad = dve.value_load(bad1[0:1, 0:1], min_val=0, max_val=P * REP)
                        with dve.If(any_bad > 0):
                            for h in range(REP):
                                rows_bad = dve.value_load(badh[0:1, h:h + 1], min_val=0, max_val=P)
                                with dve.If(rows_bad > 0):
                                    def then(ins):
                                        dve.drain()
                                    s = sc[:, p % 3, h, 0:w]
                                    dve.drain()
                                    then(v.memset(bit, 1 << 30))
                                    then(v.tensor_scalar(z0, s, 0.0, None, ALU.is_ge, ALU.add, accum_out=c))
                                    then(v.tensor_scalar(pos, c, kt, None, ALU.is_ge))
                                    then(v.tensor_scalar(one, c, kt, None, ALU.is_lt))
                                    then(v.tensor_scalar(sign, one, 31, None, ALU.logical_shift_left))
                                    then(v.tensor_copy(cur, sign))
                                    with dve.Fori(0, 31) as _:
                                        then(v.tensor_tensor(cand, cur, bit, ALU.bitwise_or))
                                        then(v.tensor_scalar(z0, s, cand.bitcast(F32), None, ALU.is_ge, ALU.add, accum_out=c))
                                        then(v.tensor_scalar(mask, c, kt, pos, ALU.is_ge, ALU.is_equal))
                                        then(v.tensor_scalar(mask, mask, 31, 31, ALU.logical_shift_left,
                                                             ALU.arith_shift_right))
                                        then(v.tensor_tensor(mask, mask, bit, ALU.bitwise_and))
                                        then(v.tensor_tensor(cur, cur, mask, ALU.bitwise_or))
                                        then(v.tensor_scalar(bit, bit, 1, None, ALU.logical_shift_right))
                                    then(v.tensor_tensor(cand, cur, one, ALU.add))
                                    t = cand.bitcast(F32)
                                    then(v.tensor_scalar(z0, s, t, None, ALU.is_gt, ALU.add, accum_out=cgt))
                                    then(v.tensor_scalar(r, cgt, -1.0, kt, ALU.mult, ALU.add))
                                    then(v.tensor_scalar(z0, s, t, None, ALU.is_equal))
                                    then(v.tensor_tensor_scan(z1, z0, z0, 0.0, ALU.add, ALU.max))
                                    then(v.scalar_tensor_tensor(z1, z1, r, z0, ALU.is_gt, ALU.mult))
                                    then(v.scalar_tensor_tensor(s, z1, MASKED, s, ALU.mult, ALU.add))
                                    then(v.tensor_copy(tt[:, p % 2, 3, h:h + 1], t))
                            dve.drain()
                        link(v.memset(fb[:, 7:8], 0.0))

                    def probabilities(p):
                        w = width(p)
                        for h in range(REP):
                            dve.wait_ge(sm["expd"], REP * p + h + 1)
                            thr = tt[:, p % 2, 3, h:h + 1] if ORDER[p] else b.tab[:, 0, TAB_OPEN:TAB_OPEN + 1]
                            s = sc[:, p % 3, h, 0:w]
                            v.scalar_tensor_tensor(s, s, thr, ex[:, h, 0:w], ALU.is_ge, ALU.mult)\
                                .then_inc(sm["prob"], 1)
                        if ORDER[p]:
                            v.memset(fb[:, 6:7], 0.0).then_inc(sm["thr"], 1)

                    def normalise(p):
                        dve.wait_ge(sm["pv"], blocks_before[p + 1])
                        acc = psum[:, 6, 0:REP * VW].rearrange("p (h d) -> p h d", h=REP)
                        link(v.reciprocal(rec[:, p % 2, :], acc[:, :, HD]))
                        if p >= 2:
                            dve.wait_ge(written[p % 2], 16 * (p // 2))
                        v.tensor_tensor(o_sb[:, p % 2, :, :], acc[:, :, 0:HD],
                                        rec[:, p % 2, :].rearrange("p (h o) -> p h o", o=1).broadcast_to([P, REP, HD]),
                                        ALU.mult).then_inc(sm["norm"], 1)

                    for p in range(TILES + 2):
                        for h in range(REP):
                            if p < TILES:
                                evacuate(p, h)
                            if h == 0 and p >= 3:
                                normalise(p - 3)
                        if 1 <= p <= TILES:
                            if ORDER[p - 1]:
                                for h in range(REP):
                                    count(p - 1, h)
                            if ORDER[p - 1]:
                                select(p - 1)
                                fall_back(p - 1)
                            probabilities(p - 1)
                    normalise(TILES - 1)
            clear(nc, [*sm.values(), *loaded, *written])


def build(nc, x, out, dram):
    with ExitStack() as ctx:
        sb = lambda n, s, d=F32: ctx.enter_context(nc.sbuf_tensor(n, s, d))
        for name, shape in (("x1", (S, D)), ("attn", (S, D))):
            dram[name] = nc.dram_tensor(f"scratch_{name}", shape, F32, kind="Internal").ap()
        dram["qk_parts"] = nc.dram_tensor("scratch_qk_parts", (PARTS, TILES, HD, H + HKV, P), BF16, kind="Internal").ap()
        b = Names()
        b.psum = ctx.enter_context(nc.psum_tensor("banks", [P, 8, BANK], F32))
        b.eye = sb("eye", [P, P])
        b.future = sb("future", [P, P])
        b.steps = sb("steps", [P, 2 * REP * 8])
        b.tab = sb("tab", [P, TILES, TABS])
        b.eye16 = sb("eye16", [P, P], BF16)
        b.future16 = sb("future16", [P, P], BF16)
        b.ones = sb("ones", [P, P])
        b.mhalf = sb("mhalf", [P, 1])
        b.minus = sb("minus", [P, REP])
        b.router = sb("router", [P, DC, E])
        b.rbias = sb("rbias", [1, E])
        b.ebias = sb("ebias", [E, D])
        b.v_all = sb("v_all", [P, TILES, HKV, VW])
        b.t_all = sb("t_all", [P, TILES, H])
        b.slope_all = sb("slope_all", [P, TILES, H])
        phase_a(nc, b, x, dram)
        phase_b(nc, b, dram)
        phase_c(nc, b, dram, out)


def kernel(**inputs):
    import concourse.bacc as bacc
    from concourse.bass_utils import run_bass_kernel_spmd as run

    x = np.ascontiguousarray(inputs["L0_attn_hidden_states"]).reshape(S, D)
    arrays = {
        "x": x,
        "wqkv": np.ascontiguousarray(np.concatenate(
            [np.asarray(inputs[n]) for n in ("L0_attn_Wq", "L0_attn_Wk", "L0_attn_Wv")], 0).T),
        "wo": np.ascontiguousarray(np.asarray(inputs["L0_attn_Wo"]).T),
        "router": np.ascontiguousarray(np.asarray(inputs["L0_ffn_router_weight"]).T),
        "rbias": np.ascontiguousarray(inputs["L0_ffn_router_bias"]).reshape(1, E),
        "ebias": np.ascontiguousarray(inputs["L0_ffn_expert_bias"]),
        **shape_constants(),
    }
    nc = bacc.Bacc("TRN2", target_bir_lowering=False, num_devices=1)
    dram = {n: nc.dram_tensor(f"in_{n}", a.shape, F32, kind="ExternalInput").ap() for n, a in arrays.items()}
    out = nc.dram_tensor("out", (S, D), F32, kind="ExternalOutput").ap()
    build(nc, dram["x"], out, dram)
    r = run(nc, [{f"in_{n}": a for n, a in arrays.items()}], core_ids=[0])
    return np.asarray(r.results[0]["out"]).reshape(1, S, D)
```

```python
from contextlib import ExitStack
import math

import numpy as np

import concourse.bass as bass
from concourse import mybir

ALU = mybir.AluOpType
ACT = mybir.ActivationFunctionType
AX = mybir.AxisListType
F32 = mybir.dt.float32
BF16 = mybir.dt.bfloat16
I32 = mybir.dt.int32

P = 128
S, D = 2048, 1024
H, HKV, HD = 32, 8, 32
REP = H // HKV
E, TOP = 64, 8
KEEP = max(min(S, 128), S - int(S * 0.9))
THETA = 10000.0
EPS = 1e-5
SCALE = float(np.float32(1.0) / np.sqrt(np.float32(HD)))
TILES = S // P
DC = D // P
QK = (H + HKV) * HD
QKC = QK // P
QKV = QK + HKV * HD
PARTS = 3
VW = HD + 1
BANK = 512
MASKED = -2.0 ** 124
OPEN = -2.0 ** 123
WINDOW = 7
(TAB_Z, TAB_SLOPE, TAB_K, TAB_COUNT, TAB_OPEN, TAB_INVN, TABS) = range(7)
U = 2


def normal_point(p):
    lo, hi = -8.0, 8.0
    for _ in range(60):
        z = (lo + hi) / 2
        lo, hi = (z, hi) if 0.5 * (1 + math.erf(z / math.sqrt(2))) < p else (lo, z)
    return z


def shape_constants():
    inv = (np.float32(1.0) / np.float32(THETA) ** (np.arange(0, HD, 2, dtype=np.float32) / np.float32(HD)))
    angle = np.outer(np.arange(S, dtype=np.float32), inv.astype(np.float32)).astype(np.float32)
    angle = np.concatenate([angle, angle], -1)
    cos, sin = np.cos(angle), np.sin(angle)
    sin[:, :HD // 2] *= -1
    rope = np.concatenate([cos, sin], -1).astype(np.float32)
    tab = np.zeros((S, TABS), np.float32)
    for r in range(S):
        n, width = r + 1, P * (r // P + 1)
        k = min(KEEP, n)
        tab[r, TAB_K] = k
        tab[r, TAB_COUNT] = width / 2 - k
        tab[r, TAB_INVN] = 1.0 / width
        if n > KEEP:
            z = normal_point(1 - min(KEEP / (n + 0.5), 0.998))
            tab[r, TAB_Z] = z
            tab[r, TAB_SLOPE] = math.sqrt(2 * math.pi) * math.exp(z * z / 2) / n
        else:
            tab[r, TAB_OPEN] = OPEN
    eye = np.eye(P, dtype=np.float32)
    future = np.triu(np.full((P, P), MASKED, np.float32), 1)
    steps = np.tile(np.concatenate([np.tile(np.arange(8), REP), np.tile(np.arange(1, 9), REP)]), (P, 1)).astype(np.float32)
    return {"rope": rope, "tab": tab, "eye": eye, "future": future, "steps": steps}


def ffn_vector(nc, dve, link, t, sm, b):
    for j in range(2):
        nc.vector.bn_stats(b.stats[:, t, j * 6:j * 6 + 6], b.x[:, t, j * BANK:(j + 1) * BANK]).then_inc(sm["bn"], 1)
    yield
    dve.wait_ge(sm["bn"], 2 * t + 2)
    nc.vector.bn_aggr(b.mv[:, t, :], b.stats[:, t, :]).then_inc(sm["var"], 1)
    yield
    dve.wait_ge(sm["rstd"], t + 1)
    nc.vector.tensor_scalar(b.xn[:, t, :], b.x[:, t, :], b.mv[:, t, 0:1], b.rstd[:, t, 0:1],
                            ALU.subtract, ALU.mult).then_inc(sm["xn"], 1)
    yield
    dve.wait_ge(sm["logits"], t + 1)
    link(nc.vector.max(b.top[:, t, :], b.psum[:, 4 * t + 2, 0:E]))
    nc.vector.tensor_scalar(b.small[:, t, 0:1], b.top[:, t, 0:1], -1.0, None, ALU.mult).then_inc(sm["negmax"], 1)
    yield
    dve.wait_ge(sm["expd"], t + 1)
    link(nc.vector.max(b.top[:, t, :], b.e64[:, t, :]))
    nc.vector.match_replace(b.rest[:, t, :], b.top[:, t, :], b.e64[:, t, :], 0.0)
    nc.vector.tensor_reduce(b.small[:, t, 2:3], b.top[:, t, :], AX.X, ALU.add)
    link(nc.vector.reciprocal(b.small[:, t, 3:4], b.small[:, t, 1:2]))
    link(nc.vector.tensor_scalar(b.small[:, t, 4:5], b.small[:, t, 3:4], 0.5, None, ALU.mult))
    link(nc.vector.tensor_tensor(b.rest[:, t, :], b.e64[:, t, :], b.rest[:, t, :], ALU.subtract))
    nc.vector.tensor_scalar(b.mix[:, t, :], b.rest[:, t, :], b.small[:, t, 4:5], None, ALU.mult).then_inc(sm["mix"], 1)
    link(nc.vector.tensor_tensor(b.small[:, t, 5:6], b.small[:, t, 2:3], b.small[:, t, 4:5], ALU.mult))
    link(nc.vector.scalar_tensor_tensor(b.x[:, t, :], b.xn[:, t, :], b.small[:, t, 5:6], b.x[:, t, :], ALU.mult, ALU.add))
    yield
    dve.wait_ge(sm["mixed"], t + 1)
    nc.vector.tensor_tensor(b.x[:, t, :], b.x[:, t, :], bank2(b.psum, 4 * t), ALU.add).then_inc(sm["x1"], 1)
    yield


def bank2(psum, first, width=2 * BANK):
    return psum[:, first:first + 4, :].rearrange("p b n -> p (b n)")[:, 0:width]


def ffn_tensor(nc, pe, t, sm, b):
    transpose8(nc, pe, t, sm["xn"], t + 1, b, 4 * t, sm["xT"])
    yield
    pe.wait_ge(sm["xTcopy"], 2 * t + 2)
    logits = b.psum[:, 4 * t + 2, 0:E]
    for c in range(DC):
        nc.tensor.matmul(logits, b.xT[:, t, c, :], b.router[:, c, :], start=(c == 0), stop=False)
    nc.tensor.matmul(logits, b.ones[0:1, :], b.rbias[0:1, :], start=False, stop=True).then_inc(sm["logits"], 1)
    yield
    pe.wait_ge(sm["mix"], t + 1)
    nc.tensor.transpose(b.psum[0:E, 4 * t + 3, 0:P], b.mix[:, t, :], b.eye[:, :]).then_inc(sm["mixT"], 1)
    yield
    pe.wait_ge(sm["mixTcopy"], t + 1)
    for j in range(2):
        last = nc.tensor.matmul(b.psum[:, 4 * t + j, :], b.mixT[:, t, :], b.ebias[:, j * BANK:(j + 1) * BANK],
                                start=True, stop=True)
    last.then_inc(sm["mixed"], 1)
    yield


def transpose8(nc, pe, t, ready, count, b, bank, done):
    pe.wait_ge(ready, count)
    for c in range(DC):
        last = nc.tensor.transpose(b.psum[:, bank + c // 4, (c % 4) * P:(c % 4 + 1) * P],
                                   b.xn[:, t, c * P:(c + 1) * P], b.eye[:, :])
    last.then_inc(done, 1)


def ffn_scalar(nc, act, t, sm, b):
    act.wait_ge(sm["xT"], t + 1)
    copy_xT(nc, t, b, 4 * t, sm["xTcopy"])
    yield
    act.wait_ge(sm["negmax"], t + 1)
    nc.scalar.activation(b.e64[:, t, :], b.psum[:, 4 * t + 2, 0:E], ACT.Exp, bias=b.small[:, t, 0:1],
                         accum_out=b.small[:, t, 1:2]).then_inc(sm["expd"], 1)
    yield
    act.wait_ge(sm["mixT"], t + 1)
    nc.scalar.activation(b.mixT[:, t, :], b.psum[0:E, 4 * t + 3, 0:P], ACT.Copy).then_inc(sm["mixTcopy"], 1)
    yield


def copy_xT(nc, t, b, bank, done):
    for j in range(2):
        nc.scalar.activation(b.xT[:, t, 4 * j:4 * j + 4, :].rearrange("p c n -> p (c n)"),
                             b.psum[:, bank + j, :], ACT.Copy).then_inc(done, 1)


def rstd_pool(nc, pool, t, var, count, done, b):
    plink = b.plink
    pool.wait_ge(var, count)
    v, r, a = b.pw[:, t, 0:1], b.pw[:, t, 1:2], b.pw[:, t, 2:3]
    plink(nc.gpsimd.tensor_scalar(v, b.mv[:, t, 1:2], EPS, None, ALU.add))
    plink(nc.gpsimd.tensor_tensor(r, v, b.mhalf[:, 0:1], ALU.pow))
    plink(nc.gpsimd.tensor_tensor(a, r, r, ALU.mult))
    plink(nc.gpsimd.tensor_tensor(a, a, v, ALU.mult))
    plink(nc.gpsimd.tensor_scalar(a, a, -0.5, 1.5, ALU.mult, ALU.add))
    nc.gpsimd.tensor_tensor(b.rstd[:, t, 0:1], r, a, ALU.mult).then_inc(done, 1)


def interleave(parts):
    parts = list(parts)
    while parts:
        parts = [p for p in parts if next(p, "end") != "end"]


def flat(x):
    return x.rearrange("p c n -> p (c n)")


class Names:
    pass


def semaphores(nc, ctx, names, prefix):
    return {n: ctx.enter_context(nc.semaphore(f"{prefix}_{n}")) for n in names.split()}


def clear(nc, sems):
    nc.all_engine_barrier()
    for s in sems:
        nc.gpsimd.sem_clear(s)
    nc.all_engine_barrier()


def linker(engine, sem):
    count = [0]

    def link(ins):
        count[0] += 1
        ins.then_inc(sem, 1)
        engine.wait_ge(sem, count[0])
    return link


def ffn_buffers(nc, ctx, b, phase):
    sb = lambda n, s, d=F32: ctx.enter_context(nc.sbuf_tensor(f"{phase}_{n}", s, d))
    b.x = sb("x", [P, U, D])
    b.xn = sb("xn", [P, U, D])
    b.xT = sb("xT", [P, U, DC, P])
    b.stats = sb("stats", [P, U, 12])
    b.mv = sb("mv", [P, U, 2])
    b.rstd = sb("rstd", [P, U, 1])
    b.pw = sb("pw", [P, U, 4])
    b.small = sb("small", [P, U, 8])
    b.top = sb("top", [P, U, TOP])
    b.e64 = sb("e64", [P, U, E])
    b.rest = sb("rest", [P, U, E])
    b.mix = sb("mix", [P, U, E])
    b.mixT = sb("mixT", [E, U, P])
    b.router = sb("router", [P, DC, E])
    b.rbias = sb("rbias", [1, E])
    b.ebias = sb("ebias", [E, D])


def load_router(sp, b, dram, loaded):
    sp.dma_start(b.router[:, :, :], dram["router"].rearrange("(c p) e -> p c e", p=P)).then_inc(loaded, 16)
    sp.dma_start(b.ebias[:, :], dram["ebias"]).then_inc(loaded, 16)
    sp.dma_start(b.rbias[:, :], dram["rbias"]).then_inc(loaded, 16)


FFN_SEMS = "x bn var rstd xn xT xTcopy logits negmax expd mix mixT mixTcopy mixed x1 vchain pchain out "


def phase_a(nc, b, x_dram, dram):
    with ExitStack() as ctx:
        sb = lambda n, s, d=F32: ctx.enter_context(nc.sbuf_tensor(n, s, d))
        ffn_buffers(nc, ctx, b, "a")
        wqkv = sb("wqkv", [P, DC, QKV])
        rope = sb("rope", [P, U, 2 * HD])
        tab = sb("tab_a", [P, U, TABS])
        future = sb("future", [P, P])
        rot = sb("rot", [P, U, H + HKV, HD])
        qk = sb("qk", [P, U, H + HKV, HD])
        qkT = sb("qkT", [P, U, QKC, P])
        krep = sb("krep", [P, U, HKV, REP, HD], BF16)
        k1 = sb("k1", [P, U, HKV, VW], BF16)
        moments16 = sb("moments16", [P, U, HKV, VW], BF16)
        moments = sb("moments", [P, U, HKV, VW])
        prod = sb("prod", [P, U, H, HD])
        sums = sb("sums", [P, U, 2, H])
        gs = sb("gs", [P, U, 4, H])
        parts = sb("parts", [P, U, PARTS, QKC, P], BF16)
        left = sb("left", [P, U, QKC, P])

        su = semaphores(nc, ctx, "w fill", "sa")
        with nc.Block() as block:
            @block.sync
            def _(sp):
                sp.dma_start(wqkv[:, :, :], dram["wqkv"].rearrange("(c p) n -> p c n", p=P)).then_inc(su["w"], 16)
                load_router(sp, b, dram, su["w"])
                sp.dma_start(b.eye[:, :], dram["eye"]).then_inc(su["w"], 16)
                sp.dma_start(future[:, :], dram["future"]).then_inc(su["w"], 16)
                sp.dma_start(b.steps[:, :], dram["steps"]).then_inc(su["w"], 16)
                sp.dma_start(b.tab[:, :, :], dram["tab"].rearrange("(t p) c -> p t c", p=P)).then_inc(su["w"], 16)
                sp.wait_ge(su["w"], 8 * 16)

            @block.vector
            def _(dve):
                nc.vector.memset(b.ones[:, :], 1.0)
                nc.vector.memset(b.mhalf[:, :], -0.5)
                nc.vector.memset(b.minus[:, :], -1.0)
                nc.vector.memset(b.tiny[:, :], 2.0 ** -126)
                nc.vector.memset(moments[:, :, :, :], 0.0)
                nc.vector.memset(b.v_all[:, :, :, :], 1.0)
                nc.vector.memset(k1[:, :, :, :], 1.0).then_inc(su["fill"], 1)
                dve.wait_ge(su["w"], 8 * 16)
                nc.vector.tensor_copy(b.eye16[:, :], b.eye[:, :])
                nc.vector.tensor_copy(b.future16[:, :], future[:, :])

        with nc.Fori(0, TILES // U) as it, ExitStack() as ctx2:
            sm = semaphores(nc, ctx2, FFN_SEMS + "tabs x1out var2 rstd2 h hT hTcopy qkv cosd sind vcopy rot qkT "
                            "qkTcopy kk mom momsum y prod sums guess high left middle low deviation momcopy", "a")
            loaded = [ctx2.enter_context(nc.semaphore(f"a_load{t}")) for t in range(U)]
            with nc.Block() as block:
                @block.sync
                def _(sp):
                    for t in range(U):
                        rows = bass.ds((it * U + t) * P, P)
                        sp.dma_start(b.x[:, t, :], x_dram[rows, :]).then_inc(loaded[t], 16)
                        sp.dma_start(rope[:, t, :], dram["rope"][rows, :]).then_inc(loaded[t], 16)
                        sp.dma_start(tab[:, t, :], dram["tab"][rows, :]).then_inc(loaded[t], 16)
                    for t in range(U):
                        rows = bass.ds((it * U + t) * P, P)
                        sp.wait_ge(sm["x1"], t + 1)
                        sp.dma_start(dram["x1"][rows, :], b.x[:, t, :]).then_inc(sm["x1out"], 16)
                    for t in range(U):
                        for part, done in enumerate(("high", "middle", "low")):
                            sp.wait_ge(sm[done], (3 * t + 3) if part == 0 else t + 1)
                            for r in range(REP):
                                sp.dma_start(dram["qk_parts"][part, it * U + t, :, r::REP, :],
                                             parts[r * HD:(r + 1) * HD, t, part, :, :]).then_inc(sm["out"], 16)
                    sp.wait_ge(sm["x1out"], 16 * U)
                    sp.wait_ge(sm["out"], 16 * U * PARTS * REP)

                @block.tensor
                def _(pe):
                    def tile(t):
                        yield from ffn_tensor(nc, pe, t, sm, b)
                        transpose8(nc, pe, t, sm["h"], t + 1, b, 4 * t + 2, sm["hT"])
                        yield
                        pe.wait_ge(sm["hTcopy"], 2 * t + 2)
                        pe.wait_ge(sm["x1"], t + 1)
                        for c in range(DC):
                            for j in range(QKV // BANK):
                                last = nc.tensor.matmul(b.psum[:, 4 * t + j, :], b.xT[:, t, c, :],
                                                        wqkv[:, c, j * BANK:(j + 1) * BANK],
                                                        start=(c == 0), stop=(c == DC - 1))
                        last.then_inc(sm["qkv"], 1)
                        yield
                        pe.wait_ge(sm["rot"], t + 1)
                        pe.wait_ge(sm["vcopy"], t + 1)
                        for c in range(QKC):
                            last = nc.tensor.transpose(
                                b.psum[:, 4 * t + c // 4, (c % 4) * P:(c % 4 + 1) * P],
                                qk[:, t, 4 * c:4 * c + 4, :].rearrange("p h d -> p (h d)"), b.eye[:, :])
                        last.then_inc(sm["qkT"], 1)
                        yield
                        pe.wait_ge(sm["kk"], t + 1)
                        for g in range(HKV):
                            last = nc.tensor.matmul(b.psum[:, 4 * t + 3, g * VW:(g + 1) * VW],
                                                    krep[:, t, g, :, :].rearrange("p r d -> p (r d)"),
                                                    k1[:, t, g, :], start=True, stop=True)
                        last.then_inc(sm["mom"], 1)
                        yield
                        pe.wait_ge(sm["momcopy"], t + 1)
                        pe.wait_ge(sm["high"], 3 * t + 3)
                        for g in range(HKV):
                            for r in range(REP):
                                q = slice(r * HD, (r + 1) * HD)
                                last = nc.tensor.matmul(b.psum[:, 4 * t + r, g * VW:(g + 1) * VW], parts[q, t, 0, g, :],
                                                        moments16[q, t, g, :], start=True, stop=True)
                        last.then_inc(sm["y"], 1)
                        yield
                    interleave(tile(t) for t in range(U))

                @block.scalar
                def _(act):
                    def tile(t):
                        yield from ffn_scalar(nc, act, t, sm, b)
                        act.wait_ge(sm["hT"], t + 1)
                        act.wait_ge(sm["logits"], t + 1)
                        copy_xT(nc, t, b, 4 * t + 2, sm["hTcopy"])
                        yield
                        act.wait_ge(sm["qkv"], t + 1)
                        act.wait_ge(sm["sind"], 3 * t + 3)
                        nc.scalar.activation(b.v_all[:, it * U + t, :, 0:HD],
                                             b.psum[:, 4 * t + 2, 256:512].rearrange("p (g d) -> p g d", g=HKV),
                                             ACT.Copy).then_inc(sm["vcopy"], 1)
                        yield
                        act.wait_ge(sm["qkT"], t + 1)
                        for j, c in enumerate((0, 4, 8)):
                            w = min(4, QKC - c)
                            nc.scalar.activation(qkT[:, t, c:c + w, :].rearrange("p c n -> p (c n)"),
                                                 b.psum[:, 4 * t + j, 0:w * P], ACT.Copy).then_inc(sm["qkTcopy"], 1)
                            nc.scalar.activation(parts[:, t, 0, c:c + w, :].rearrange("p c n -> p (c n)"),
                                                 b.psum[:, 4 * t + j, 0:w * P], ACT.Copy).then_inc(sm["high"], 1)
                        yield
                        act.wait_ge(sm["left"], t + 1)
                        nc.scalar.activation(flat(parts[:, t, 1, :, :]), flat(left[:, t, :, :]), ACT.Copy)\
                            .then_inc(sm["middle"], 1)
                        yield
                    interleave(tile(t) for t in range(U))

                @block.gpsimd
                def _(pool):
                    b.plink = plink = linker(pool, sm["pchain"])

                    def tile(t):
                        rstd_pool(nc, pool, t, sm["var"], t + 1, sm["rstd"], b)
                        yield
                        pool.wait_ge(sm["xn"], t + 1)
                        rstd_pool(nc, pool, t, sm["var2"], t + 1, sm["rstd2"], b)
                        yield
                        pool.wait_ge(sm["rot"], t + 1)
                        for r in range(REP):
                            nc.gpsimd.tensor_copy(krep[:, t, :, r, :], qk[:, t, H:, :])
                        nc.gpsimd.tensor_copy(k1[:, t, :, 0:HD], qk[:, t, H:, :]).then_inc(sm["kk"], 1)
                        yield
                        pool.wait_ge(sm["deviation"], t + 1)
                        mean, sq, t0, sl = (gs[:, t, j, :] for j in range(4))
                        col = lambda c: tab[:, t, c:c + 1]
                        plink(nc.gpsimd.tensor_scalar(t0, sq, col(TAB_Z), None, ALU.mult))
                        plink(nc.gpsimd.tensor_tensor(t0, t0, mean, ALU.add))
                        plink(nc.gpsimd.tensor_scalar(t0, t0, col(TAB_OPEN), None, ALU.add))
                        plink(nc.gpsimd.tensor_scalar(sl, sq, col(TAB_SLOPE), None, ALU.mult))
                        nc.gpsimd.tensor_copy(b.t_all[:, it * U + t, :], t0)
                        nc.gpsimd.tensor_copy(b.slope_all[:, it * U + t, :], sl).then_inc(sm["guess"], 1)
                        yield
                    interleave(tile(t) for t in range(U))

                @block.vector
                def _(dve):
                    link = linker(dve, sm["vchain"])

                    def tile(t):
                        dve.wait_ge(loaded[t], 48)
                        yield from ffn_vector(nc, dve, link, t, sm, b)
                        dve.wait_ge(sm["x1"], t + 1)
                        for j in range(2):
                            last = nc.vector.bn_stats(b.stats[:, t, j * 6:j * 6 + 6],
                                                      b.x[:, t, j * BANK:(j + 1) * BANK])
                            if j:
                                link(last)
                        nc.vector.bn_aggr(b.mv[:, t, :], b.stats[:, t, :]).then_inc(sm["var2"], 1)
                        yield
                        dve.wait_ge(sm["rstd2"], t + 1)
                        dve.wait_ge(sm["xT"], t + 1)
                        nc.vector.tensor_scalar(b.xn[:, t, :], b.x[:, t, :], b.mv[:, t, 0:1], b.rstd[:, t, 0:1],
                                                ALU.subtract, ALU.mult).then_inc(sm["h"], 1)
                        yield
                        dve.wait_ge(sm["qkv"], t + 1)
                        proj = bank2(b.psum, 4 * t, QK).rearrange("p (h d) -> p h d", d=HD)
                        lo, hi = slice(0, HD // 2), slice(HD // 2, HD)
                        cos = rope[:, t:t + 1, 0:HD].broadcast_to([P, H + HKV, HD])
                        sin = rope[:, t:t + 1, HD:2 * HD]
                        nc.vector.tensor_tensor(qk[:, t, :, :], proj, cos, ALU.mult).then_inc(sm["sind"], 1)
                        nc.vector.tensor_tensor(rot[:, t, :, lo], proj[:, :, hi],
                                                sin[:, :, lo].broadcast_to([P, H + HKV, HD // 2]),
                                                ALU.mult).then_inc(sm["sind"], 1)
                        nc.vector.tensor_tensor(rot[:, t, :, hi], proj[:, :, lo],
                                                sin[:, :, hi].broadcast_to([P, H + HKV, HD // 2]),
                                                ALU.mult).then_inc(sm["sind"], 1)
                        dve.wait_ge(sm["sind"], 3 * t + 3)
                        nc.vector.tensor_tensor(qk[:, t, :, :], qk[:, t, :, :], rot[:, t, :, :],
                                                ALU.add).then_inc(sm["rot"], 1)
                        yield
                        dve.wait_ge(sm["high"], 3 * t + 3)
                        nc.vector.tensor_tensor(flat(left[:, t, :, :]), flat(qkT[:, t, :, :]),
                                                flat(parts[:, t, 0, :, :]), ALU.subtract).then_inc(sm["left"], 1)
                        yield
                        dve.wait_ge(sm["middle"], t + 1)
                        nc.vector.tensor_tensor(flat(parts[:, t, 2, :, :]), flat(left[:, t, :, :]),
                                                flat(parts[:, t, 1, :, :]), ALU.subtract).then_inc(sm["low"], 1)
                        dve.wait_ge(sm["mom"], t + 1)
                        if t:
                            dve.wait_ge(sm["momsum"], t)
                        nc.vector.tensor_tensor(moments[:, t, :, :], moments[:, 1 - t, :, :],
                                                b.psum[:, 4 * t + 3, 0:HKV * VW].rearrange("p (g d) -> p g d", g=HKV),
                                                ALU.add).then_inc(sm["momsum"], 1)
                        dve.wait_ge(sm["momsum"], t + 1)
                        nc.vector.tensor_copy(moments16[:, t, :, :], moments[:, t, :, :]).then_inc(sm["momcopy"], 1)
                        yield
                        dve.wait_ge(sm["y"], t + 1)
                        for r in range(REP):
                            y = b.psum[:, 4 * t + r, 0:HKV * VW].rearrange("p (g d) -> p g d", g=HKV)
                            copied = nc.vector.tensor_copy(sums[:, t, 1, r::REP], y[:, :, HD])
                            last = nc.vector.tensor_tensor(prod[:, t, r::REP, :], y[:, :, 0:HD], qk[:, t, r:H:REP, :],
                                                           ALU.mult)
                        copied.then_inc(sm["sums"], 1)
                        link(last)
                        link(nc.vector.tensor_reduce(sums[:, t, 0, :], prod[:, t, :, :], AX.X, ALU.add))
                        dve.wait_ge(sm["sums"], t + 1)
                        e2, s1 = sums[:, t, 0, :], sums[:, t, 1, :]
                        mean, sq, var, half = (gs[:, t, j, :] for j in range(4))
                        n = tab[:, t, TAB_INVN:TAB_INVN + 1]
                        link(nc.vector.tensor_scalar(mean, s1, n, None, ALU.mult))
                        link(nc.vector.tensor_tensor(sq, mean, mean, ALU.mult))
                        link(nc.vector.scalar_tensor_tensor(var, e2, n, sq, ALU.mult, ALU.subtract))
                        link(nc.vector.tensor_scalar(var, var, 1e-30, None, ALU.max))
                        link(nc.vector.tensor_scalar(sq.bitcast(I32), var.bitcast(I32), 0.5, float(0x1FBD0000),
                                                     ALU.mult, ALU.add))
                        for last in (False, True):
                            link(nc.vector.reciprocal(half, sq))
                            link(nc.vector.tensor_tensor(half, half, var, ALU.mult))
                            link(nc.vector.tensor_tensor(half, half, sq, ALU.add))
                            step = nc.vector.tensor_scalar(sq, half, 0.5, None, ALU.mult)
                            if last:
                                step.then_inc(sm["deviation"], 1)
                            else:
                                link(step)
                        yield
                    interleave(tile(t) for t in range(U))
            clear(nc, [*sm.values(), *loaded])


def phase_c(nc, b, dram, out):
    with ExitStack() as ctx:
        sb = lambda n, s, d=F32: ctx.enter_context(nc.sbuf_tensor(n, s, d))
        ffn_buffers(nc, ctx, b, "c")
        wo = sb("wo", [P, DC, D])
        su = semaphores(nc, ctx, "w", "sc")
        with nc.Block() as block:
            @block.sync
            def _(sp):
                sp.dma_start(wo[:, :, :], dram["wo"].rearrange("(c p) n -> p c n", p=P)).then_inc(su["w"], 16)
                load_router(sp, b, dram, su["w"])
                sp.wait_ge(su["w"], 4 * 16)

        with nc.Fori(0, TILES // U) as it, ExitStack() as ctx2:
            sm = semaphores(nc, ctx2, FFN_SEMS + "aT aTcopy proj xsum", "c")
            loaded = [ctx2.enter_context(nc.semaphore(f"c_load{t}")) for t in range(U)]
            with nc.Block() as block:
                @block.sync
                def _(sp):
                    for t in range(U):
                        rows = bass.ds((it * U + t) * P, P)
                        sp.dma_start(b.xn[:, t, :], dram["attn"][rows, :]).then_inc(loaded[t], 16)
                        sp.dma_start(b.x[:, t, :], dram["x1"][rows, :]).then_inc(loaded[t], 16)
                    for t in range(U):
                        rows = bass.ds((it * U + t) * P, P)
                        sp.wait_ge(sm["x1"], t + 1)
                        sp.dma_start(out[rows, :], b.x[:, t, :]).then_inc(sm["out"], 16)
                    sp.wait_ge(sm["out"], 16 * U)

                @block.tensor
                def _(pe):
                    def tile(t):
                        transpose8(nc, pe, t, loaded[t], 32, b, 4 * t + 2, sm["aT"])
                        yield
                        pe.wait_ge(sm["aTcopy"], 2 * t + 2)
                        for c in range(DC):
                            for j in range(2):
                                last = nc.tensor.matmul(b.psum[:, 4 * t + j, :], b.xT[:, t, c, :],
                                                        wo[:, c, j * BANK:(j + 1) * BANK],
                                                        start=(c == 0), stop=(c == DC - 1))
                        last.then_inc(sm["proj"], 1)
                        yield
                        yield from ffn_tensor(nc, pe, t, sm, b)
                    interleave(tile(t) for t in range(U))

                @block.scalar
                def _(act):
                    def tile(t):
                        act.wait_ge(sm["aT"], t + 1)
                        copy_xT(nc, t, b, 4 * t + 2, sm["aTcopy"])
                        yield
                        act.wait_ge(sm["proj"], t + 1)
                        yield from ffn_scalar(nc, act, t, sm, b)
                    interleave(tile(t) for t in range(U))

                @block.gpsimd
                def _(pool):
                    b.plink = linker(pool, sm["pchain"])

                    def tile(t):
                        rstd_pool(nc, pool, t, sm["var"], t + 1, sm["rstd"], b)
                        yield
                    interleave(tile(t) for t in range(U))

                @block.vector
                def _(dve):
                    link = linker(dve, sm["vchain"])

                    def tile(t):
                        dve.wait_ge(loaded[t], 32)
                        dve.wait_ge(sm["proj"], t + 1)
                        link(nc.vector.tensor_tensor(b.x[:, t, :], b.x[:, t, :], bank2(b.psum, 4 * t), ALU.add))
                        yield
                        yield from ffn_vector(nc, dve, link, t, sm, b)
                    interleave(tile(t) for t in range(U))
            clear(nc, [*sm.values(), *loaded])


GROUPS = 2
ORDER = list(range(TILES)) + list(range(TILES - 1, -1, -1))
GROUP = [0] * TILES + [1] * TILES
PLACES = len(ORDER)


def uses_of_slots():
    return [(p, h, c, min(2 * BANK, P * (i + 1) - 2 * BANK * c))
            for p, i in enumerate(ORDER) for h in range(REP) for c in range(-(-P * (i + 1) // (2 * BANK)))]


QUAD = 32

AMONG = 0.2
TURNED = (4, 5, 7)
LAG = 2
NEXT_SCORES = 0.8

SCALAR_STEPS = ("exp0 exp1 first0 first1 first2 first3 diff0 diff1 exp2 diff2 diff3 "
                "second0 second1 second2 second3 exp3 third0 third1 third2 third3")
COPYING = 11

ONE_BITS = 0x3F800000

Q_ROWS = ((0, 0, 1, 1), (0, 2, 1, 2))
K_ROWS = ((0, 1, 0, 1), (2, 0, 2, 1))


def phase_b(nc, b, dram):
    uses = uses_of_slots()
    evacuated = {}
    for n, (p, h, c, w) in enumerate(uses):
        evacuated[p, h] = n + 1
    chosen = [sum(i > 0 for i in ORDER[:p]) for p in range(PLACES + 1)]
    chunks = [-(-P * (i + 1) // (2 * BANK)) for i in ORDER]
    blocks_before = [sum(ORDER[q] + 1 for q in range(p)) for p in range(PLACES + 1)]

    with ExitStack() as ctx:
        sb = lambda n, s, d=F32: ctx.enter_context(nc.sbuf_tensor(n, s, d))
        q_sb = sb("q_sb", [P, 2, 2, REP, P], BF16)
        k_sb = sb("k_sb", [P, 2, TILES, P], BF16)
        v_sb = sb("v_sb", [P, TILES, GROUPS, VW])
        tg = sb("tg", [P, TILES, GROUPS * REP])
        slg = sb("slg", [P, TILES, GROUPS * REP])
        sc = sb("sc", [P, 3, REP, S])
        ex = sb("ex", [P, REP, S])
        keys = sb("keys", [P, 2, S])
        nt3 = sb("nt3", [P, 2, REP])
        junk = sb("junk", [P, 2, S], BF16)
        passed = sb("passed", [P, S], BF16)
        pT = sb("pT", [P, 4, REP * P])
        mx = sb("mx", [P, 3, 2, REP])
        nmx = sb("nmx", [P, 2, REP])
        sgn = sb("sgn", [P, 2, 3, REP])
        tt = sb("tt", [P, 2, 4, REP])
        dd = sb("dd", [P, 2, 3, REP])
        pw = sb("pw_b", [P, 8, REP])
        cnt = sb("cnt", [P, 2, REP])
        d = sb("d", [P, REP])
        js = sb("js", [P, 6, REP])
        sel = sb("sel", [P, 2, REP, 8])
        dirn = sb("dirn", [P, REP], I32)
        flip = sb("flip", [P, REP], I32)
        near = sb("near", [P, REP, 8])
        pick = sb("pick", [P, 2, REP, 8])
        dk = sb("dk", [P, 2, REP])
        gap = sb("gap", [P, 4, REP])
        bad = sb("bad", [P, QUAD])
        badT = sb("badT", [P, QUAD])
        quads = sb("quads", [P, P // QUAD])
        heads_bad = sb("heads_bad", [QUAD, QUAD])
        heads_row = sb("heads_row", [QUAD, QUAD])
        rec = sb("rec", [P, 2, REP])
        o_sb = sb("o_sb", [P, 2, REP, HD])
        fb = sb("fb", [P, 8])
        fbi = sb("fbi", [P, 8], I32)
        psum = b.psum

        def slot(n):
            return bank2(psum, 2 * (n % 2))

        def width(p):
            return P * (ORDER[p] + 1)

        def wide(x):
            return x.rearrange("p (h o) -> p h o", o=1).broadcast_to([P, REP, 8])

        def share(p, low, high):
            nb = ORDER[p] + 1
            return range(round(nb * low), round(nb * high))

        def heads_of(p):
            return slice(GROUP[p] * REP, (GROUP[p] + 1) * REP)

        with nc.Fori(0, HKV // GROUPS) as it, ExitStack() as ctx2:
            sm = semaphores(nc, ctx2, "k vt s evac nmx t1 t2 t3 expd nt3 diff key vchain pchain dist thr sel prob pT "
                            "pTcopy pv norm junk", "b")
            loaded = [ctx2.enter_context(nc.semaphore(f"b_q{n}")) for n in range(2)]
            written = [ctx2.enter_context(nc.semaphore(f"b_written{n}")) for n in range(2)]
            with nc.Block() as block:
                def store(sp, p):
                    sp.wait_ge(sm["norm"], p + 1)
                    sp.dma_start(dram["attn"][ORDER[p] * P:(ORDER[p] + 1) * P, bass.ds((it * GROUPS + GROUP[p]) * P, P)],
                                 o_sb[:, p % 2, :, :].rearrange("p h d -> p (h d)")).then_inc(written[p % 2], 16)

                @block.sync
                def _(sp):
                    parts = dram["qk_parts"]

                    def load_q(p):
                        if p >= 2:
                            sp.wait_ge(sm["s"], evacuated[p - 2, REP - 1])
                        for m in range(2):
                            for r in range(4):
                                sp.dma_start(q_sb[r * HD:(r + 1) * HD, p % 2, m, :, :],
                                             parts[Q_ROWS[m][r], ORDER[p], :, bass.ds((it * GROUPS + GROUP[p]) * REP, REP), :])\
                                    .then_inc(loaded[p % 2], 16)

                    def load_k(group):
                        for m in range(2):
                            for r in range(4):
                                sp.dma_start(k_sb[r * HD:(r + 1) * HD, m, :, :],
                                             parts[K_ROWS[m][r], :, :, bass.ds(it * GROUPS + (group + H), 1), :]
                                             .rearrange("t d o s -> d t (o s)")).then_inc(sm["k"], 16)

                    load_q(0)
                    load_k(0)
                    load_q(1)
                    for p in range(PLACES):
                        if p + 1 < PLACES and GROUP[p + 1] != GROUP[p]:
                            sp.wait_ge(sm["s"], evacuated[p, REP - 1])
                            load_k(GROUP[p + 1])
                        if p + 2 < PLACES:
                            load_q(p + 2)
                        if p >= 3:
                            store(sp, p - 3)
                    for p in range(PLACES - 3, PLACES):
                        store(sp, p)
                    for w in written:
                        sp.wait_ge(w, 16 * PLACES // 2)

                @block.tensor
                def _(pe):

                    def scores(p, h):
                        if h == 0:
                            if p == 0 or GROUP[p] != GROUP[p - 1]:
                                pe.wait_ge(sm["k"], 16 * 8 * (GROUP[p] + 1))
                            pe.wait_ge(loaded[p % 2], 16 * 8 * (p // 2 + 1))
                        for n, (pp, hh, c, w) in enumerate(uses):
                            if (pp, hh) != (p, h):
                                continue
                            if n >= 2:
                                pe.wait_ge(sm["evac"], n - 1)
                            for j in range(0, w, BANK):
                                wj = min(BANK, w - j)
                                col = c * 2 * BANK + j
                                diag = col + wj == width(p)
                                for m in range(2):
                                    last = nc.tensor.matmul(slot(n)[:, j:j + wj], q_sb[:, p % 2, m, h, :],
                                                            flat(k_sb[:, m, :, :])[:, col:col + wj],
                                                            start=(m == 0), stop=(m == 1 and not diag))
                                if diag:
                                    last = nc.tensor.matmul(slot(n)[:, j + wj - P:j + wj], b.eye16[:, :],
                                                            b.future16[:, :], start=False, stop=True)
                            last.then_inc(sm["s"], 1)

                    def turn(p, kb):
                        n = blocks_before[p] + kb
                        if n >= 3:
                            pe.wait_ge(sm["pTcopy"], n - 2)
                        for h in range(REP):
                            last = nc.tensor.transpose(psum[:, TURNED[n % 3], h * P:(h + 1) * P],
                                                       sc[:, p % 3, h, kb * P:(kb + 1) * P], b.eye[:, :])
                        last.then_inc(sm["pT"], 1)

                    def product(p, kb):
                        n = blocks_before[p] + kb
                        pe.wait_ge(sm["pTcopy"], n + 1)
                        if kb == 0 and p == 0:
                            pe.wait_ge(sm["vt"], 3)
                        if kb == 0 and p:
                            pe.wait_ge(sm["norm"], p)
                        for h in range(REP):
                            last = nc.tensor.matmul(psum[:, 6, h * VW:(h + 1) * VW],
                                                    pT[:, n % 4, h * P:(h + 1) * P], v_sb[:, kb, GROUP[p], :],
                                                    start=(kb == 0 and h == 0), stop=(kb == ORDER[p]),
                                                    skip_group_check=True)
                        last.then_inc(sm["pv"], 1)

                    def values(p, blocks):
                        for kb in blocks:
                            turn(p, kb)
                            if kb >= LAG:
                                product(p, kb - LAG)

                    for p in range(PLACES + 2):
                        for h in range(REP):
                            if p < PLACES and (h or p == 0):
                                scores(p, h)
                            if p >= 2:
                                if h == 0:
                                    pe.wait_ge(sm["prob"], REP * (p - 1))
                                values(p - 2, share(p - 2, AMONG * h / REP, AMONG * (h + 1) / REP))
                        if p >= 2:
                            values(p - 2, share(p - 2, AMONG, NEXT_SCORES))
                        if p + 1 < PLACES:
                            scores(p + 1, 0)
                        if p >= 2:
                            values(p - 2, share(p - 2, NEXT_SCORES, 1))
                            for kb in range(max(ORDER[p - 2] + 1 - LAG, 0), ORDER[p - 2] + 1):
                                product(p - 2, kb)

                @block.scalar
                def _(act):
                    signs = [0]
                    act.wait_ge(sm["vt"], 1)

                    def count(p, h, k, t):
                        n = signs[0]
                        signs[0] += 1
                        if n >= 2:
                            act.wait_ge(sm["junk"], n - 1)
                        w = width(p)
                        nc.scalar.activation(junk[:, n % 2, 0:w], sc[:, p % 3, h, 0:w], ACT.Sign, bias=t, scale=-1.0,
                                             accum_out=sgn[:, p % 2, k, h:h + 1]).then_inc(sm["junk"], 1)

                    def exponential(p, h):
                        if h == 0:
                            act.wait_ge(sm["nmx"], p + 1)
                        if p:
                            act.wait_ge(sm["prob"], REP * (p - 1) + h + 1)
                        w = width(p)
                        nc.scalar.activation(ex[:, h, 0:w], sc[:, p % 3, h, 0:w], ACT.Exp,
                                             bias=nmx[:, p % 2, h:h + 1], scale=SCALE).then_inc(sm["expd"], 1)

                    def difference(p, h):
                        n = REP * chosen[p] + h
                        if h == 0:
                            act.wait_ge(sm["nt3"], chosen[p + 1])
                            if chosen[p]:
                                act.wait_ge(sm["thr"], chosen[p])
                        if n >= 2:
                            act.wait_ge(sm["key"], n - 1)
                        w = width(p)
                        nc.scalar.activation(keys[:, n % 2, 0:w], sc[:, p % 3, h, 0:w], ACT.Identity,
                                             bias=nt3[:, p % 2, h:h + 1]).then_inc(sm["diff"], 1)

                    def copies(p, low, high):
                        if p < 0:
                            return
                        for kb in share(p, low, high):
                            n = blocks_before[p] + kb
                            act.wait_ge(sm["pT"], n + 1)
                            if n >= 4:
                                act.wait_ge(sm["pv"], n - 3)
                            nc.scalar.activation(pT[:, n % 4, :], psum[:, TURNED[n % 3], :], ACT.Copy)\
                                .then_inc(sm["pTcopy"], 1)

                    for p in range(PLACES + 2):
                        new = p < PLACES and ORDER[p]
                        steps = SCALAR_STEPS.split()
                        last_first = steps.index(f"first{REP - 1}")
                        for n, step in enumerate(steps):
                            kind, h = step[:-1], int(step[-1])
                            if kind == "exp" and 1 <= p <= PLACES:
                                exponential(p - 1, h)
                            elif kind == "diff" and 1 <= p <= PLACES and ORDER[p - 1]:
                                difference(p - 1, h)
                            elif kind == "first":
                                if new:
                                    act.wait_ge(sm["evac"], evacuated[p, h])
                                    count(p, h, 0, tg[:, ORDER[p], GROUP[p] * REP + h:GROUP[p] * REP + h + 1])
                                copies(p - 2, AMONG * h / REP, AMONG * (h + 1) / REP)
                            elif kind in ("second", "third") and new:
                                k = 1 if kind == "second" else 2
                                if h == 0:
                                    act.wait_ge(sm[f"t{k}"], chosen[p + 1])
                                count(p, h, k, tt[:, p % 2, k - 1, h:h + 1])
                            m = n - last_first - 1
                            if m >= 0:
                                copies(p - 2, AMONG + (1 - AMONG) * min(m / COPYING, 1),
                                       AMONG + (1 - AMONG) * min((m + 1) / COPYING, 1))

                @block.gpsimd
                def _(pool):
                    link = linker(pool, sm["pchain"])
                    gp = nc.gpsimd
                    both = bass.ds(it * (GROUPS * REP), GROUPS * REP)
                    gp.tensor_copy(tg[:, :, :], b.t_all[:, :, both]).then_inc(sm["vt"], 1)
                    gp.tensor_copy(slg[:, :, :], b.slope_all[:, :, both]).then_inc(sm["vt"], 1)
                    gp.tensor_copy(v_sb[:, :, :, :], b.v_all[:, :, bass.ds(it * GROUPS, GROUPS), :])\
                        .then_inc(sm["vt"], 1)
                    pool.wait_ge(sm["vt"], 3)

                    def update(p, k, done):
                        i = ORDER[p]
                        before = tg[:, i, heads_of(p)] if k == 0 else tt[:, p % 2, k - 1, :]
                        dist = dd[:, p % 2, k, :]
                        st = slg[:, i, heads_of(p)]
                        gate, move, den, s, lo = (pw[:, j, :] for j in range(5))
                        link(gp.tensor_scalar(dist, sgn[:, p % 2, k, :], -0.5, b.tab[:, i, TAB_COUNT:TAB_COUNT + 1],
                                              ALU.mult, ALU.add))
                        link(gp.tensor_tensor(gate, dist, dist, ALU.mult))
                        link(gp.tensor_scalar(gate, gate, (WINDOW - 0.4) ** 2, None, ALU.is_gt))
                        if k == 0:
                            link(gp.tensor_tensor(move, dist, st, ALU.mult))
                        else:
                            older = tg[:, i, heads_of(p)] if k == 1 else tt[:, p % 2, k - 2, :]
                            link(gp.tensor_tensor(den, dd[:, p % 2, k - 1, :], dist, ALU.subtract))
                            link(gp.tensor_tensor(s, before, older, ALU.subtract))
                            link(gp.tensor_tensor(s, s, den, ALU.mult))
                            link(gp.tensor_tensor(den, den, den, ALU.mult))
                            link(gp.tensor_scalar(den, den, 0.25, None, ALU.max))
                            link(gp.tensor_scalar(lo, st, 1e-30, None, ALU.max))
                            link(gp.tensor_tensor(den, den, lo, ALU.mult))
                            link(gp.tensor_tensor(den, den, b.minus[:, :], ALU.pow))
                            link(gp.tensor_tensor(s, s, den, ALU.mult))
                            link(gp.tensor_scalar(s, s, 0.5, 2.0, ALU.max, ALU.min))
                            link(gp.tensor_tensor(s, s, st, ALU.mult))
                            link(gp.tensor_tensor(move, dist, s, ALU.mult))
                        link(gp.tensor_tensor(move, move, gate, ALU.mult))
                        gp.tensor_tensor(tt[:, p % 2, k, :], before, move, ALU.add).then_inc(done, 1)
                        if k == 2:
                            pool.wait_ge(done, chosen[p + 1])
                            gp.tensor_scalar(nt3[:, p % 2, :], tt[:, p % 2, k, :], -1.0, None, ALU.mult)\
                                .then_inc(sm["nt3"], 1)

                    def selectors(p):
                        pool.wait_ge(sm["dist"], chosen[p + 1])
                        if chosen[p]:
                            pool.wait_ge(sm["sel"], 2 * chosen[p])
                        a, j1, j2, nz, x = (js[:, j, :] for j in range(5))
                        steps = [b.steps[:, m * REP * 8:(m + 1) * REP * 8].rearrange("p (h o) -> p h o", h=REP)
                                 for m in range(2)]
                        link(gp.tensor_scalar(x, d[:, :], 0.0, None, ALU.is_ge))
                        link(gp.tensor_scalar(x, x, 2.0, -1.0, ALU.mult, ALU.add))
                        link(gp.tensor_tensor(a, d[:, :], x, ALU.mult))
                        link(gp.tensor_scalar(x, x, 0.5, -0.5, ALU.mult, ALU.add))
                        link(gp.tensor_tensor(j1, a, x, ALU.add))
                        link(gp.tensor_scalar(j2, a, 2.0, None, ALU.mult))
                        link(gp.tensor_tensor(j2, j2, j1, ALU.subtract))
                        link(gp.tensor_scalar(nz, a, 0.0, None, ALU.is_gt))
                        for m, j in enumerate((j1, j2)):
                            e = sel[:, m, :, :]
                            link(gp.tensor_tensor(e, steps[m], wide(j), ALU.subtract))
                            link(gp.tensor_scalar(e, e, 0.0, None, ALU.is_equal))
                            gp.tensor_tensor(e, e, wide(nz), ALU.mult).then_inc(sm["sel"], 1)

                    rounds = 0
                    for p in range(PLACES + 1):
                        if p < PLACES:
                            pool.wait_ge(sm["evac"], evacuated[p, REP - 1])
                            if p >= 2:
                                pool.wait_ge(sm["expd"], REP * (p - 1))
                            gp.tensor_scalar(nmx[:, p % 2, :], mx[:, p % 3, chunks[p] - 1, :], -SCALE, None,
                                             ALU.mult).then_inc(sm["nmx"], 1)
                        new = p < PLACES and ORDER[p]
                        if new:
                            if p >= 2 and chosen[p - 1]:
                                pool.wait_ge(sm["thr"], chosen[p - 1])
                            rounds += REP
                            pool.wait_ge(sm["junk"], rounds)
                            update(p, 0, sm["t1"])
                        if p and ORDER[p - 1]:
                            selectors(p - 1)
                        if new:
                            for k, done in ((1, sm["t2"]), (2, sm["t3"])):
                                rounds += REP
                                pool.wait_ge(sm["junk"], rounds)
                                update(p, k, done)

                @block.vector
                def _(dve):
                    link = linker(dve, sm["vchain"])
                    v = nc.vector
                    v.memset(bad[:, :], 0.0)
                    link(v.memset(heads_bad[:, :], 0.0))

                    def evacuate(p, h):
                        for n, (pp, hh, c, w) in enumerate(uses):
                            if (pp, hh) != (p, h):
                                continue
                            dve.wait_ge(sm["s"], n + 1)
                            if p >= 3 and h == 0 and c == 0:
                                dve.wait_ge(sm["nmx"], p - 2)
                                dve.wait_ge(sm["pT"], blocks_before[p - 2])
                            if c:
                                dve.wait_ge(sm["evac"], n)
                            v.tensor_scalar(sc[:, p % 3, h, c * 2 * BANK:c * 2 * BANK + w], slot(n)[:, 0:w], 0.0,
                                            mx[:, p % 3, 0, h:h + 1] if c else None, ALU.add, ALU.max,
                                            accum_out=mx[:, p % 3, c, h:h + 1]).then_inc(sm["evac"], 1)

                    def count(p, h):
                        if h == 0:
                            dve.wait_ge(sm["t3"], chosen[p + 1])
                        w = width(p)
                        link(v.tensor_scalar(passed[:, 0:w], sc[:, p % 3, h, 0:w], tt[:, p % 2, 2, h:h + 1],
                                             None, ALU.is_ge, ALU.add, accum_out=cnt[:, p % 2, h:h + 1]))

                    def select(p):
                        i, w = ORDER[p], width(p)
                        t3 = tt[:, p % 2, 2, :]
                        kt = b.tab[:, i, TAB_K:TAB_K + 1]
                        if chosen[p]:
                            dve.wait_ge(sm["sel"], 2 * chosen[p])
                        v.tensor_scalar(d[:, :], cnt[:, p % 2, :], kt, None, ALU.subtract).then_inc(sm["dist"], 1)
                        dve.wait_ge(sm["dist"], chosen[p + 1])
                        link(v.tensor_scalar(dirn[:, :], d[:, :], 0.0, None, ALU.is_gt))
                        link(v.tensor_scalar(flip[:, :], dirn[:, :], 29, 0x1FFFFFFF, ALU.logical_shift_left,
                                             ALU.bitwise_or))
                        for h in range(REP):
                            z = keys[:, h % 2, 0:w]
                            dve.wait_ge(sm["diff"], REP * chosen[p] + h + 1)
                            link(v.tensor_scalar(z.bitcast(I32), z.bitcast(I32), 2, flip[:, h:h + 1],
                                                 ALU.logical_shift_right, ALU.bitwise_xor))
                            v.max(near[:, h, :], z).then_inc(sm["key"], 1)
                        dve.wait_ge(sm["key"], REP * chosen[p + 1])
                        bits = near[:, :, :].bitcast(I32)
                        link(v.tensor_tensor(bits, bits, wide(flip[:, :]), ALU.bitwise_xor))
                        link(v.tensor_scalar(bits, bits, 2, None, ALU.logical_shift_left))
                        dve.wait_ge(sm["sel"], 2 * chosen[p + 1])
                        twice = near[:, :, :].rearrange("p (o h) e -> p o (h e)", o=1).broadcast_to([P, 2, REP * 8])
                        link(v.tensor_tensor(pick[:, :, :, :].rearrange("p o h e -> p o (h e)"),
                                             sel[:, :, :, :].rearrange("p o h e -> p o (h e)"), twice, ALU.mult))
                        link(v.tensor_reduce(dk[:, :, :], pick[:, :, :, :], AX.X, ALU.add))
                        kth, nxt = dk[:, 0, :], dk[:, 1, :]
                        g0, g1, g2, g3 = (gap[:, j, :] for j in range(4))
                        link(v.tensor_tensor(g0, kth, nxt, ALU.subtract))
                        link(v.tensor_scalar(g1, g0, 2.0 ** 100, -2.0 ** 19, ALU.min, ALU.mult))
                        link(v.tensor_tensor(g2, g1, kth, ALU.subtract))
                        link(v.tensor_tensor(g1, g1, kth, ALU.add))
                        link(v.tensor_tensor(g1, g1, g2, ALU.max))
                        link(v.tensor_scalar(g1, g1, 0.0, None, ALU.is_ge))
                        link(v.tensor_tensor(g2, d[:, :], d[:, :], ALU.mult))
                        link(v.scalar_tensor_tensor(g1, g2, 0.5, g1, ALU.is_gt, ALU.mult))
                        link(v.scalar_tensor_tensor(bad[:, 1:1 + REP], g2, (WINDOW + 0.5) ** 2, g1, ALU.is_gt,
                                                    ALU.max))
                        link(v.tensor_reduce(bad[:, 0:1], bad[:, 1:1 + REP], AX.X, ALU.max))
                        link(v.scalar_tensor_tensor(g3, g0, -0.25, kth, ALU.mult, ALU.add))
                        link(v.tensor_tensor(tt[:, p % 2, 3, :], t3, g3, ALU.add))

                    def fall_back(p):
                        i, w = ORDER[p], width(p)
                        kt = b.tab[:, i, TAB_K:TAB_K + 1]
                        link(v.transpose(badT[:, :], bad[:, :]))
                        link(v.tensor_reduce(quads[:, 0:1], badT[:, :], AX.X, ALU.max))
                        for n in range(1, P // QUAD):
                            moved = v.tensor_copy(quads[0:QUAD, n:n + 1], quads[n * QUAD:(n + 1) * QUAD, 0:1])
                        link(moved)
                        link(v.tensor_reduce(heads_bad[:, 0:1], quads[0:QUAD, :], AX.X, ALU.max))
                        c, pos, cgt, r = (fb[:, j:j + 1] for j in range(4))
                        cur, bit, cand, sign, mask, one = (fbi[:, j:j + 1] for j in range(6))
                        z0, z1 = passed[:, 0:w], keys[:, 0, 0:w]
                        any_bad = dve.value_load(heads_bad[0:1, 0:1].bitcast(I32), min_val=0, max_val=ONE_BITS)
                        with dve.If(any_bad > 0):
                            dve.wait_ge(sm["expd"], REP * p + REP)
                            v.transpose(heads_row[:, :], heads_bad[:, :])
                            dve.drain()
                            for h in range(REP):
                                rows_bad = dve.value_load(heads_row[0:1, 1 + h:2 + h].bitcast(I32), min_val=0,
                                                          max_val=ONE_BITS)
                                with dve.If(rows_bad > 0):
                                    def then(ins):
                                        dve.drain()
                                    s = sc[:, p % 3, h, 0:w]
                                    dve.drain()
                                    then(v.memset(bit, 1 << 30))
                                    then(v.tensor_scalar(z0, s, 0.0, None, ALU.is_ge, ALU.add, accum_out=c))
                                    then(v.tensor_scalar(pos, c, kt, None, ALU.is_ge))
                                    then(v.tensor_scalar(one, c, kt, None, ALU.is_lt))
                                    then(v.tensor_scalar(sign, one, 31, None, ALU.logical_shift_left))
                                    then(v.tensor_copy(cur, sign))
                                    with dve.Fori(0, 31) as _:
                                        then(v.tensor_tensor(cand, cur, bit, ALU.bitwise_or))
                                        then(v.tensor_scalar(z0, s, cand.bitcast(F32), None, ALU.is_ge, ALU.add, accum_out=c))
                                        then(v.tensor_scalar(mask, c, kt, pos, ALU.is_ge, ALU.is_equal))
                                        then(v.tensor_scalar(mask, mask, 31, 31, ALU.logical_shift_left,
                                                             ALU.arith_shift_right))
                                        then(v.tensor_tensor(mask, mask, bit, ALU.bitwise_and))
                                        then(v.tensor_tensor(cur, cur, mask, ALU.bitwise_or))
                                        then(v.tensor_scalar(bit, bit, 1, None, ALU.logical_shift_right))
                                    then(v.tensor_tensor(cand, cur, one, ALU.add))
                                    t = cand.bitcast(F32)
                                    then(v.tensor_scalar(z0, s, t, None, ALU.is_gt, ALU.add, accum_out=cgt))
                                    then(v.tensor_scalar(r, cgt, -1.0, kt, ALU.mult, ALU.add))
                                    then(v.tensor_scalar(z0, s, t, None, ALU.is_equal))
                                    then(v.tensor_tensor_scan(z1, z0, z0, 0.0, ALU.add, ALU.max))
                                    then(v.scalar_tensor_tensor(z1, z1, r, z0, ALU.is_gt, ALU.mult))
                                    then(v.scalar_tensor_tensor(s, z1, MASKED, s, ALU.mult, ALU.add))
                                    then(v.tensor_copy(tt[:, p % 2, 3, h:h + 1], t))
                            dve.drain()
                        link(v.memset(fb[:, 7:8], 0.0))

                    def probabilities(p):
                        w = width(p)
                        for h in range(REP):
                            dve.wait_ge(sm["expd"], REP * p + h + 1)
                            thr = tt[:, p % 2, 3, h:h + 1] if ORDER[p] else b.tab[:, 0, TAB_OPEN:TAB_OPEN + 1]
                            s = sc[:, p % 3, h, 0:w]
                            v.scalar_tensor_tensor(s, s, thr, ex[:, h, 0:w], ALU.is_ge, ALU.mult)\
                                .then_inc(sm["prob"], 1)
                        if ORDER[p]:
                            v.memset(fb[:, 6:7], 0.0).then_inc(sm["thr"], 1)

                    def normalise(p):
                        dve.wait_ge(sm["pv"], blocks_before[p + 1])
                        acc = psum[:, 6, 0:REP * VW].rearrange("p (h d) -> p h d", h=REP)
                        link(v.reciprocal(rec[:, p % 2, :], acc[:, :, HD]))
                        if p >= 2:
                            dve.wait_ge(written[p % 2], 16 * (p // 2))
                        v.tensor_tensor(o_sb[:, p % 2, :, :], acc[:, :, 0:HD],
                                        rec[:, p % 2, :].rearrange("p (h o) -> p h o", o=1).broadcast_to([P, REP, HD]),
                                        ALU.mult).then_inc(sm["norm"], 1)

                    for p in range(PLACES + 2):
                        for h in range(REP):
                            if p < PLACES:
                                evacuate(p, h)
                            if h == 0 and p >= 3:
                                normalise(p - 3)
                        if 1 <= p <= PLACES:
                            if ORDER[p - 1]:
                                for h in range(REP):
                                    count(p - 1, h)
                            if ORDER[p - 1]:
                                select(p - 1)
                                fall_back(p - 1)
                            probabilities(p - 1)
                    normalise(PLACES - 1)
            clear(nc, [*sm.values(), *loaded, *written])


def build(nc, x, out, dram):
    with ExitStack() as ctx:
        sb = lambda n, s, d=F32: ctx.enter_context(nc.sbuf_tensor(n, s, d))
        for name, shape in (("x1", (S, D)), ("attn", (S, D))):
            dram[name] = nc.dram_tensor(f"scratch_{name}", shape, F32, kind="Internal").ap()
        dram["qk_parts"] = nc.dram_tensor("scratch_qk_parts", (PARTS, TILES, HD, H + HKV, P), BF16, kind="Internal").ap()
        b = Names()
        b.psum = ctx.enter_context(nc.psum_tensor("banks", [P, 8, BANK], F32))
        b.eye = sb("eye", [P, P])
        b.steps = sb("steps", [P, 2 * REP * 8])
        b.tab = sb("tab", [P, TILES, TABS])
        b.eye16 = sb("eye16", [P, P], BF16)
        b.future16 = sb("future16", [P, P], BF16)
        b.ones = sb("ones", [P, P])
        b.mhalf = sb("mhalf", [P, 1])
        b.minus = sb("minus", [P, REP])
        b.tiny = sb("tiny", [P, 1])
        b.v_all = sb("v_all", [P, TILES, HKV, VW])
        b.t_all = sb("t_all", [P, TILES, H])
        b.slope_all = sb("slope_all", [P, TILES, H])
        phase_a(nc, b, x, dram)
        phase_b(nc, b, dram)
        phase_c(nc, b, dram, out)


def kernel(**inputs):
    import concourse.bacc as bacc
    from concourse.bass_utils import run_bass_kernel_spmd as run

    x = np.ascontiguousarray(inputs["L0_attn_hidden_states"]).reshape(S, D)
    arrays = {
        "x": x,
        "wqkv": np.ascontiguousarray(np.concatenate(
            [np.asarray(inputs[n]) for n in ("L0_attn_Wq", "L0_attn_Wk", "L0_attn_Wv")], 0).T),
        "wo": np.ascontiguousarray(np.asarray(inputs["L0_attn_Wo"]).T),
        "router": np.ascontiguousarray(np.asarray(inputs["L0_ffn_router_weight"]).T),
        "rbias": np.ascontiguousarray(inputs["L0_ffn_router_bias"]).reshape(1, E),
        "ebias": np.ascontiguousarray(inputs["L0_ffn_expert_bias"]),
        **shape_constants(),
    }
    nc = bacc.Bacc("TRN2", target_bir_lowering=False, num_devices=1)
    dram = {n: nc.dram_tensor(f"in_{n}", a.shape, F32, kind="ExternalInput").ap() for n, a in arrays.items()}
    out = nc.dram_tensor("out", (S, D), F32, kind="ExternalOutput").ap()
    build(nc, dram["x"], out, dram)
    r = run(nc, [{f"in_{n}": a for n, a in arrays.items()}], core_ids=[0])
    return np.asarray(r.results[0]["out"]).reshape(1, S, D)
```
